# Optimizing a Trainium2 kernel written in Bass

```python
import numpy as np
import jax
import jax.numpy as jnp

def _softmax(x, axis=-1):
    return jax.nn.softmax(x, axis=axis)

def _gelu(x):
    return jax.nn.gelu(x, approximate=True)

def _silu(x):
    return jax.nn.silu(x)

def _sigmoid(x):
    return jax.nn.sigmoid(x)

def _layernorm(x, axis=-1, eps=1e-05):
    m = jnp.mean(x, axis=axis, keepdims=True)
    v = jnp.var(x, axis=axis, keepdims=True)
    return (x - m) / jnp.sqrt(v + eps)

def _scatter_add(tgt, idx, src, axis=0):
    return tgt.at[idx].add(src)

def _segment_sum(src, seg, n):
    return jax.ops.segment_sum(src, seg, n)
kernel_name = 'mk_conv_preact_d2_conv_nhwc384_r2_5b3025'

def setup_inputs(seed: int=0):
    np.random.seed(seed)
    _w = jnp.asarray

    def _rec_inputs():
        import jax
        import jax.numpy as jnp
        _gk = jax.random.key(seed)
        x = -0.000357 + 1 * jax.random.normal(jax.random.fold_in(_gk, 1), (16, 56, 56, 192), jnp.float32)
        return x
    x = _rec_inputs()

    def _L0_conv_setup():
        import jax, jax.numpy as jnp
        import numpy as np
        WS = 7
        EPS = 1e-05

        def _ln(x, w, b):
            mu = jnp.mean(x, axis=-1, keepdims=True)
            var = jnp.mean((x - mu) ** 2, axis=-1, keepdims=True)
            return (x - mu) / jnp.sqrt(var + EPS) * w + b

        def _mamba(xw, A, Bm, Cm):
            xB = xw @ Bm
            xs = jnp.swapaxes(xB, 0, 1)

            def step(h, xb):
                h = xb + h @ A
                return (h, h)
            h0 = jnp.zeros_like(xs[0])
            _, hs = jax.lax.scan(step, h0, xs)
            h = jnp.swapaxes(hs, 0, 1)
            return h @ Cm
        key = jax.random.key(seed)
        ks = jax.random.split(key, 12)
        dim = 192
        hid = 4 * dim
        s = 1.0 / np.sqrt(dim)
        d = {}
        d['x'] = jax.random.normal(ks[0], (16, 56, 56, dim), jnp.float32)
        d['A'] = jax.random.normal(ks[1], (dim, dim), jnp.float32) * (1.0 / dim)
        d['Bm'] = jax.random.normal(ks[2], (dim, dim), jnp.float32) * s
        d['Cm'] = jax.random.normal(ks[3], (dim, dim), jnp.float32) * s
        d['ln1_w'] = jnp.ones((dim,), jnp.float32)
        d['ln1_b'] = jnp.zeros((dim,), jnp.float32)
        d['ln2_w'] = jnp.ones((dim,), jnp.float32)
        d['ln2_b'] = jnp.zeros((dim,), jnp.float32)
        d['W1'] = jax.random.normal(ks[4], (dim, hid), jnp.float32) * s
        d['b1'] = jnp.zeros((hid,), jnp.float32)
        d['W2'] = jax.random.normal(ks[5], (hid, dim), jnp.float32) * (1.0 / np.sqrt(hid))
        d['b2'] = jnp.zeros((dim,), jnp.float32)
        return d
    _L0_conv_all = _L0_conv_setup()
    _L0_conv_in = {k: v for k, v in _L0_conv_all.items() if k in ('A', 'Bm', 'Cm', 'ln1_w', 'ln1_b', 'ln2_w', 'ln2_b', 'W1', 'b1', 'W2', 'b2')}
    del _L0_conv_all

    def _L1_conv_setup():
        import jax, jax.numpy as jnp
        import numpy as np
        WH, WW = (7, 7)
        S0, S1 = (3, 3)
        NH = 12
        C = 192

        def _rel_pos_index(wh, ww):
            coords = np.stack(np.meshgrid(np.arange(wh), np.arange(ww), indexing='ij')).reshape(2, -1)
            rel = coords[:, :, None] - coords[:, None, :]
            rel = rel.transpose(1, 2, 0).astype(np.int64)
            rel[..., 0] += wh - 1
            rel[..., 1] += ww - 1
            rel[..., 0] *= 2 * ww - 1
            return rel.sum(-1)

        def _shift_mask(ph, pw, wh, ww, s0, s1):
            img = np.zeros((ph, pw), dtype=np.float32)
            cnt = 0
            for hs in ((0, ph - wh), (ph - wh, ph - s0), (ph - s0, ph)):
                for ws in ((0, pw - ww), (pw - ww, pw - s1), (pw - s1, pw)):
                    img[hs[0]:hs[1], ws[0]:ws[1]] = cnt
                    cnt += 1
            win = img.reshape(ph // wh, wh, pw // ww, ww).transpose(0, 2, 1, 3).reshape(-1, wh * ww)
            diff = win[:, None, :] - win[:, :, None]
            return np.where(diff != 0, -100.0, 0.0).astype(np.float32)
        key = jax.random.key(seed)
        ks = jax.random.split(key, 6)
        return {'x': jax.random.normal(ks[0], (32, 56, 56, C), jnp.float32), 'qkv_w': jax.random.normal(ks[1], (3 * C, C), jnp.float32) * 0.02, 'qkv_b': jax.random.normal(ks[2], (3 * C,), jnp.float32) * 0.02, 'proj_w': jax.random.normal(ks[3], (C, C), jnp.float32) * 0.02, 'proj_b': jax.random.normal(ks[4], (C,), jnp.float32) * 0.02, 'rpb_table': jax.random.normal(ks[5], ((2 * WH - 1) * (2 * WW - 1), NH), jnp.float32) * 0.02}
    _L1_conv_all = _L1_conv_setup()
    _L1_conv_in = {k: v for k, v in _L1_conv_all.items() if k in ('qkv_w', 'qkv_b', 'proj_w', 'proj_b', 'rpb_table')}
    del _L1_conv_all
    return {'x': x, 'L0_conv_A': _L0_conv_in['A'], 'L0_conv_Bm': _L0_conv_in['Bm'], 'L0_conv_Cm': _L0_conv_in['Cm'], 'L0_conv_ln1_w': _L0_conv_in['ln1_w'], 'L0_conv_ln1_b': _L0_conv_in['ln1_b'], 'L0_conv_ln2_w': _L0_conv_in['ln2_w'], 'L0_conv_ln2_b': _L0_conv_in['ln2_b'], 'L0_conv_W1': _L0_conv_in['W1'], 'L0_conv_b1': _L0_conv_in['b1'], 'L0_conv_W2': _L0_conv_in['W2'], 'L0_conv_b2': _L0_conv_in['b2'], 'L1_conv_qkv_w': _L1_conv_in['qkv_w'], 'L1_conv_qkv_b': _L1_conv_in['qkv_b'], 'L1_conv_proj_w': _L1_conv_in['proj_w'], 'L1_conv_proj_b': _L1_conv_in['proj_b'], 'L1_conv_rpb_table': _L1_conv_in['rpb_table']}

def reference(x, L0_conv_A, L0_conv_Bm, L0_conv_Cm, L0_conv_ln1_w, L0_conv_ln1_b, L0_conv_ln2_w, L0_conv_ln2_b, L0_conv_W1, L0_conv_b1, L0_conv_W2, L0_conv_b2, L1_conv_qkv_w, L1_conv_qkv_b, L1_conv_proj_w, L1_conv_proj_b, L1_conv_rpb_table):
    import jax
    import jax.numpy as jnp

    def _L0_conv_ref(x, A, Bm, Cm, ln1_w, ln1_b, ln2_w, ln2_b, W1, b1, W2, b2):
        import jax, jax.numpy as jnp
        import numpy as np
        WS = 7
        EPS = 1e-05

        def _ln(x, w, b):
            mu = jnp.mean(x, axis=-1, keepdims=True)
            var = jnp.mean((x - mu) ** 2, axis=-1, keepdims=True)
            return (x - mu) / jnp.sqrt(var + EPS) * w + b

        def _mamba(xw, A, Bm, Cm):
            xB = xw @ Bm
            xs = jnp.swapaxes(xB, 0, 1)

            def step(h, xb):
                h = xb + h @ A
                return (h, h)
            h0 = jnp.zeros_like(xs[0])
            _, hs = jax.lax.scan(step, h0, xs)
            h = jnp.swapaxes(hs, 0, 1)
            return h @ Cm
        Bn, H, W, C = x.shape
        ws = WS
        w = x.reshape(Bn, H // ws, ws, W // ws, ws, C)
        w = w.transpose(0, 1, 3, 2, 4, 5).reshape(-1, ws * ws, C)
        w = _ln(w, ln1_w, ln1_b)
        w = _mamba(w, A, Bm, Cm)
        xr = w.reshape(Bn, H // ws, W // ws, ws, ws, C)
        xr = xr.transpose(0, 1, 3, 2, 4, 5).reshape(Bn, H, W, C)
        y = _ln(xr, ln2_w, ln2_b)
        y = jax.nn.gelu(y @ W1 + b1, approximate=False) @ W2 + b2
        return xr + y

    def _L1_conv_ref(x, qkv_w, qkv_b, proj_w, proj_b, rpb_table):
        import jax, jax.numpy as jnp
        import numpy as np
        WH, WW = (7, 7)
        S0, S1 = (3, 3)
        NH = 12
        C = 192

        def _rel_pos_index(wh, ww):
            coords = np.stack(np.meshgrid(np.arange(wh), np.arange(ww), indexing='ij')).reshape(2, -1)
            rel = coords[:, :, None] - coords[:, None, :]
            rel = rel.transpose(1, 2, 0).astype(np.int64)
            rel[..., 0] += wh - 1
            rel[..., 1] += ww - 1
            rel[..., 0] *= 2 * ww - 1
            return rel.sum(-1)

        def _shift_mask(ph, pw, wh, ww, s0, s1):
            img = np.zeros((ph, pw), dtype=np.float32)
            cnt = 0
            for hs in ((0, ph - wh), (ph - wh, ph - s0), (ph - s0, ph)):
                for ws in ((0, pw - ww), (pw - ww, pw - s1), (pw - s1, pw)):
                    img[hs[0]:hs[1], ws[0]:ws[1]] = cnt
                    cnt += 1
            win = img.reshape(ph // wh, wh, pw // ww, ww).transpose(0, 2, 1, 3).reshape(-1, wh * ww)
            diff = win[:, None, :] - win[:, :, None]
            return np.where(diff != 0, -100.0, 0.0).astype(np.float32)
        b, h, w, c = x.shape
        pad_b, pad_r = (-h % WH, -w % WW)
        x = jnp.pad(x, ((0, 0), (0, pad_b), (0, pad_r), (0, 0)))
        ph, pw = (h + pad_b, w + pad_r)
        s0 = 0 if WH >= ph else S0
        s1 = 0 if WW >= pw else S1
        if s0 + s1 > 0:
            x = jnp.roll(x, (-s0, -s1), axis=(1, 2))
        nwh, nww = (ph // WH, pw // WW)
        nw = nwh * nww
        N = WH * WW
        hd = c // NH
        xw = x.reshape(b, nwh, WH, nww, WW, c).transpose(0, 1, 3, 2, 4, 5).reshape(b * nw, N, c)
        qkv = xw @ qkv_w.T + qkv_b
        qkv = qkv.reshape(b * nw, N, 3, NH, hd).transpose(2, 0, 3, 1, 4)
        q, k, v = (qkv[0] * hd ** (-0.5), qkv[1], qkv[2])
        attn = jnp.einsum('bhnd,bhmd->bhnm', q, k)
        rel_idx = _rel_pos_index(WH, WW)
        bias = rpb_table[rel_idx.reshape(-1)].reshape(N, N, NH).transpose(2, 0, 1)
        attn = attn + bias[None]
        if s0 + s1 > 0:
            mask = jnp.asarray(_shift_mask(ph, pw, WH, WW, s0, s1))
            attn = attn.reshape(b, nw, NH, N, N) + mask[None, :, None]
            attn = attn.reshape(b * nw, NH, N, N)
        attn = jax.nn.softmax(attn, axis=-1)
        out = jnp.einsum('bhnm,bhmd->bhnd', attn, v).transpose(0, 2, 1, 3).reshape(b * nw, N, c)
        out = out @ proj_w.T + proj_b
        out = out.reshape(b, nwh, nww, WH, WW, c).transpose(0, 1, 3, 2, 4, 5).reshape(b, ph, pw, c)
        if s0 + s1 > 0:
            out = jnp.roll(out, (s0, s1), axis=(1, 2))
        return out[:, :h, :w, :]

    def _gn(v, G=32, eps=1e-05):
        B_, H_, W_, C_ = v.shape
        g = v.reshape(B_, H_, W_, G, C_ // G)
        m = jnp.mean(g, axis=(1, 2, 4), keepdims=True)
        s = jnp.var(g, axis=(1, 2, 4), keepdims=True)
        return ((g - m) / jnp.sqrt(s + eps)).reshape(v.shape)

    def _ln_c(v, eps=1e-06):
        m = jnp.mean(v, axis=-1, keepdims=True)
        s = jnp.var(v, axis=-1, keepdims=True)
        return (v - m) / jnp.sqrt(s + eps)

    def _ln_t(v, eps=1e-05):
        m = jnp.mean(v, axis=-1, keepdims=True)
        s = jnp.var(v, axis=-1, keepdims=True)
        return (v - m) / jnp.sqrt(s + eps)

    def _to_tokens(v):
        B_, H_, W_, C_ = v.shape
        return v.reshape(B_, H_ * W_, C_)

    def _from_tokens(t, like):
        return t.reshape(like.shape)
    x = x + _L0_conv_ref(_gn(x), L0_conv_A, L0_conv_Bm, L0_conv_Cm, L0_conv_ln1_w, L0_conv_ln1_b, L0_conv_ln2_w, L0_conv_ln2_b, L0_conv_W1, L0_conv_b1, L0_conv_W2, L0_conv_b2)
    x = x + _L1_conv_ref(_gn(x), L1_conv_qkv_w, L1_conv_qkv_b, L1_conv_proj_w, L1_conv_proj_b, L1_conv_rpb_table)
    return x

_drawn_inputs = setup_inputs


def setup_inputs(seed=0):
    import zlib

    import numpy as np

    out = dict(_drawn_inputs(seed))
    spreads = {'L0_conv_ln1_w': (1.0, 0.2),
     'L0_conv_ln1_b': (0.0, 0.1),
     'L0_conv_ln2_w': (1.0, 0.2),
     'L0_conv_ln2_b': (0.0, 0.1),
     'L0_conv_b1': (0.0, 0.1),
     'L0_conv_b2': (0.0, 0.1)}
    factors = {'L1_conv_qkv_w': 4.542,
     'L1_conv_qkv_b': 8.0,
     'L1_conv_proj_w': 4.567,
     'L1_conv_proj_b': 4.679,
     'L1_conv_rpb_table': 8.0}
    for name, (base, spread) in spreads.items():
        noise = np.random.default_rng([zlib.crc32(name.encode()), seed]).standard_normal(out[name].shape)
        drawn = base * np.exp(spread * noise) if base else spread * noise
        out[name] = jnp.asarray(drawn.astype(out[name].dtype))
    for name, factor in factors.items():
        out[name] = (out[name] * factor).astype(out[name].dtype)
    return out
```

```python
from contextlib import ExitStack

import numpy as np

import concourse.bass as bass
from concourse import mybir

fp32 = mybir.dt.float32
ALU = mybir.AluOpType
ACT = mybir.ActivationFunctionType
AX = mybir.AxisListType

IMGS, SIDE, C = 16, 56, 192
WS = 7
CELLS = SIDE // WS
WINS = CELLS * CELLS
T = WS * WS
SHIFT = 3
GROUPS, CG = 32, C // 32
HID = 4 * C
HEADS, HD = 12, 16
P = 128
HALF = C // 2
PAIRS = 3
NT = IMGS // 2
TPC = 4
CHUNKS = NT // TPC
NTOK = TPC * P
FT = HID // P
STEPS = T * CHUNKS
GN_EPS = LN_EPS = 1e-5
UNITS = CELLS * IMGS
SLOT = 64
UP = CELLS // 2
CROW = CELLS + 2


def cell_tokens():
    return [(int(i < SHIFT), int(j < SHIFT), i, j) for i in range(WS) for j in range(WS)]


def upto(engine, semaphore, count):
    if isinstance(count, int) and count <= 0:
        return
    engine.wait_ge(semaphore, count)


def build(nc, x, A, Bm, Cm, ln1, ln2, W1, b1, W2, b2,
          qkvT, qkv_b, projT, proj_b, rpb, block_mean, identity, head_masks, onehot, shift_mask, out):
    top = ExitStack()

    def sem(name):
        return top.enter_context(nc.semaphore(name))

    with top:
        x1_cells = nc.dram_tensor("x1_cells", [CROW, IMGS, CROW, T, C], fp32).ap()
        gn2_cols = nc.dram_tensor("gn2_cols", [CELLS, IMGS, HALF, 4], fp32).ap()

        def keep(name, shape):
            return top.enter_context(nc.sbuf_tensor(name, shape, fp32))

        ident = keep("ident", [P, P])
        blockm = keep("blockm", [P, P])
        neg_half = keep("neg_half", [P, 256])
        acc_x = keep("acc_x", [P, NT, C])
        acc_x2 = keep("acc_x2", [P, NT, C])

        with ExitStack() as ctx:
            def sb(name, shape):
                return ctx.enter_context(nc.sbuf_tensor(name, shape, fp32))

            def ps(name, shape):
                return ctx.enter_context(nc.psum_tensor(name, shape, fp32))

            xs = [sb(f"xs{b}", [P, T, C]) for b in range(2)]
            st = sb("st", [P, NT * GROUPS, 6])
            pm = sb("pm", [P, 2, NT * GROUPS])
            sq = sb("sq", [P, 2, NT * GROUPS])
            gmean = sb("gmean", [P, NT * GROUPS])
            gvar = sb("gvar", [P, NT * GROUPS])
            grstd = sb("grstd", [P, NT * GROUPS])
            gshift = sb("gshift", [P, NT * GROUPS])
            R1 = sb("R1", [P, NT, C])
            M1 = sb("M1", [P, NT, C])
            wA = sb("wA", [HALF, 2, C])
            wB = sb("wB", [HALF, 2, C])
            wC = sb("wC", [HALF, 2, C])
            w1 = sb("w1", [HALF, 2, HID])
            w2 = sb("w2", [P, FT, C])
            l1 = sb("l1", [HALF, 2, 2])
            l2 = sb("l2", [HALF, 2, 2])
            b1c = sb("b1c", [P, FT])
            b1f = sb("b1f", [P, FT])
            b2b = sb("b2b", [P, C])
            hbias = sb("hbias", [HALF, 2])
            wBs = sb("wBs", [HALF, 2, C])
            w1s = sb("w1s", [HALF, 2, HID])

            xt = [sb(f"xt{b}", [P, TPC, C]) for b in range(2)]
            res = [sb(f"res{b}", [P, TPC, C]) for b in range(2)]
            xn = [sb(f"xn{b}", [P, TPC, C]) for b in range(2)]
            x1 = [sb(f"x1{b}", [P, TPC, C]) for b in range(2)]
            xnT = [sb(f"xnT{b}", [HALF, 2, NTOK]) for b in range(2)]
            hT = [sb(f"hT{b}", [HALF, 2, NTOK]) for b in range(2)]
            yb = sb("yb", [P, TPC, C])
            yT = sb("yT", [HALF, 2, NTOK])
            gT = sb("gT", [P, FT, NTOK])
            x1sq = sb("x1sq", [P, TPC, C])
            s6a = sb("s6a", [P, TPC, 6])
            s6b = sb("s6b", [P, TPC, 6])
            mva = sb("mva", [P, TPC, 2])
            mvb = sb("mvb", [P, TPC, 2])
            vea = sb("vea", [P, TPC])
            veb = sb("veb", [P, TPC])
            rsa = sb("rsa", [P, TPC])
            rsb = sb("rsb", [P, TPC])

            ps_h = ps("ps_h", [P, 2, 512])
            ps_g = ps("ps_g", [P, 2, 512])
            ps_r = ps("ps_r", [P, 2, 512])
            ps_o = ps("ps_o", [P, 2, 512])

            def tok(t):
                return t[:, :, 0:2 * C]

            def tok_tile(t, k):
                return t[:, k // 2, (k % 2) * C:(k % 2 + 1) * C]

            def two(t):
                return t[:, :, :].rearrange("p (a b) c -> p a (b c)", b=2)

            s_w = sem("weights_loaded")
            s_xs = [sem(f"stat_rows_loaded{b}") for b in range(2)]
            s_bn = sem("stat_rows_used")
            s_fold = sem("folded")
            s_sum = sem("group_sums")
            s_pow = sem("group_rstd")
            s_tab = sem("group_tables")
            s_init = sem("init_done")
            s_x = [sem(f"x_loaded{b}") for b in range(2)]
            s_gs, s_gn = sem("gn_scaled"), sem("gn_done")
            s_st1, s_ag1, s_ve1 = sem("ln1_stats"), sem("ln1_aggregated"), sem("ln1_var_eps")
            s_rs1, s_xn = sem("ln1_rstd"), sem("xn_ready")
            s_t1, s_xnT = sem("xn_transposed"), sem("xnT_ready")
            s_scan, s_h = sem("scan_summed"), sem("h_ready")
            s_cm, s_res, s_rsum = sem("mixed"), sem("residual_ready"), sem("residual_summed")
            s_st2, s_ag2, s_ve2 = sem("ln2_stats"), sem("ln2_aggregated"), sem("ln2_var_eps")
            s_rs2, s_y = sem("ln2_rstd"), sem("y_ready")
            s_t2, s_yT = sem("y_transposed"), sem("yT_ready")
            s_w1, s_gelu = sem("hidden_summed"), sem("hidden_ready")
            s_w2, s_x1 = sem("mlp_summed"), sem("x1_ready")
            s_sq, s_acc1, s_acc2 = sem("x1_squared"), sem("x1_accumulated"), sem("x1_squares_accumulated")
            s_st = [sem(f"x1_stored{b}") for b in range(2)]
            STORES = 16 * 2 * (TPC + 3)

            def slots(engine, slot):
                for n in range(-2, 4):
                    slot(n // 2, n % 2)
                with engine.Fori(2, T - 1) as t:
                    slot(t, 0)
                    slot(t, 1)
                for n in range(STEPS - 2, STEPS + 1):
                    slot(n // 2, n % 2)

            def there(n):
                return not isinstance(n, int) or 0 <= n < STEPS

            block = ctx.enter_context(nc.Block())

            @block.sync
            def _(sp):
                for dst, src in ((ident[:, :], identity), (blockm[:, :], block_mean),
                                 (wA[:, :, :], A.rearrange("(h p) n -> p h n", h=2)),
                                 (wB[:, :, :], Bm.rearrange("(h p) n -> p h n", h=2)),
                                 (wC[:, :, :], Cm.rearrange("(h p) n -> p h n", h=2)),
                                 (w1[:, :, :], W1.rearrange("(h p) n -> p h n", h=2)),
                                 (w2[:, :, :], W2.rearrange("(f p) n -> p f n", p=P)),
                                 (b2b[:, :], b2.partition_broadcast(P)),
                                 (l1[:, :, :], ln1), (l2[:, :, :], ln2), (b1c[:, :], b1)):
                    sp.dma_start(dst, src).then_inc(s_w, 16)
                for k in range(NT):
                    if k >= 2:
                        sp.wait_ge(s_bn, k - 1)
                    sp.dma_start(xs[k % 2][:, :, :], x[k]).then_inc(s_xs[k % 2], 16)

                def slot(t, c):
                    n = CHUNKS * t + c
                    if there(n + 2):
                        upto(sp, s_res, n + 1)
                        sp.dma_start(xt[c][:, :, :],
                                     x[TPC * c:TPC * (c + 1), :, bass.ds(t + 1, 1), :]
                                     .rearrange("k p t c -> p k (t c)")).then_inc(s_x[c], 16)
                    if there(n - 1):
                        d, u = (1 - c), (t if c else t - 1)
                        i = u // WS
                        a, b = (WS + SHIFT - 1 - i) // WS, (WS + SHIFT - 1 - u % WS) // WS
                        sp.wait_ge(s_init, 1)
                        sp.wait_ge(s_x1, n)
                        for q in range(2):
                            imgs = slice(2 * TPC * d + q, 2 * TPC * (d + 1), 2)
                            base = q * WINS
                            rows, cols = bass.ds(1 - a, CELLS), bass.ds(1 - b, CELLS)
                            row, col = bass.ds(CELLS + 1 - a, 1), bass.ds(CELLS + 1 - b, 1)
                            parts = [(x1[d][base:base + WINS, k, :],
                                      x1_cells[rows, imgs.start + 2 * k, cols, bass.ds(u, 1), :]
                                      .rearrange("r w t c -> r w (t c)")) for k in range(TPC)]
                            parts += [(x1[d][base:base + CELLS, :, :],
                                       x1_cells[row, imgs, cols, bass.ds(u, 1), :]
                                       .rearrange("r k w t c -> (r w) k (t c)")),
                                      (x1[d][base:base + WINS:CELLS, :, :],
                                       x1_cells[rows, imgs, col, bass.ds(u, 1), :]
                                       .rearrange("r k w t c -> (r w) k (t c)")),
                                      (x1[d][base:base + 1, :, :],
                                       x1_cells[row, imgs, col, bass.ds(u, 1), :]
                                       .rearrange("r k w t c -> (r w) k (t c)"))]
                            for src, dst in parts:
                                sp.dma_start(dst, src).then_inc(s_st[d], 16)

                slots(sp, slot)
                for d in range(2):
                    sp.wait_ge(s_st[d], STORES * T)

            @block.scalar
            def _(act):
                act.wait_ge(s_init, 1)

                def slot(t, c):
                    n = CHUNKS * t + c
                    if there(n + 1):
                        act.wait_ge(s_scan, n + 2)
                        if not isinstance(n, int) or n >= 1:
                            act.wait_ge(s_cm, n)
                        for h in range(2):
                            last = act.activation(hT[1 - c][:, h, :], ps_h[0:HALF, h, :], ACT.Identity,
                                                  bias=hbias[:, h:h + 1])
                        last.then_inc(s_h, 1)
                    if there(n):
                        for f in range(FT):
                            act.wait_ge(s_w1, FT * n + f + 1)
                            if f == 0:
                                upto(act, s_w2, n)
                            act.activation(gT[:, f, :], ps_g[:, f % 2, :], ACT.Gelu,
                                           bias=b1f[:, f:f + 1]).then_inc(s_gelu, 1)
                    if there(n + 2):
                        act.wait_ge(s_t1, n + 3)
                        upto(act, s_scan, n + 1)
                        act.activation(xnT[c][:, :, :], ps_h[0:HALF, :, :], ACT.Copy).then_inc(s_xnT, 1)
                    if there(n + 1):
                        act.wait_ge(s_t2, n + 2)
                        act.activation(yT[:, :, :], ps_g[0:HALF, :, :], ACT.Copy).then_inc(s_yT, 1)

                slots(act, slot)

            @block.gpsimd
            def _(pool):
                pool.memset(neg_half[:, :], -0.5)
                pool.memset(acc_x[:, :, :], 0.0)
                for c in range(2):
                    pool.memset(hT[c][:, :, :], 0.0)
                pool.memset(acc_x2[:, :, :], 0.0).then_inc(s_init, 1)
                pool.wait_ge(s_init, 1)
                pool.wait_ge(s_fold, 11)
                pool.tensor_tensor(grstd[:, :], gvar[:, :], neg_half[:, :], ALU.pow).then_inc(s_pow, 1)

                def slot(t, c):
                    n = CHUNKS * t + c
                    if there(n + 2):
                        pool.wait_ge(s_ve1, n + 3)
                        pool.tensor_tensor(rsa[:, :], vea[:, :], neg_half[:, 0:TPC], ALU.pow).then_inc(s_rs1, 1)
                    if there(n + 1):
                        d = 1 - c
                        pool.wait_ge(s_gs, n + 2)
                        upto(pool, s_x1, n)
                        pool.tensor_tensor(res[d][:, :, :], xt[d][:, :, :],
                                           b2b[:, :].unsqueeze(1).to_broadcast([P, TPC, C]),
                                           ALU.add).then_inc(s_res, 1)
                        pool.wait_ge(s_ve2, n + 2)
                        pool.tensor_tensor(rsb[:, :], veb[:, :], neg_half[:, 0:TPC], ALU.pow).then_inc(s_rs2, 1)
                    if there(n - 1):
                        d = 1 - c
                        pool.wait_ge(s_x1, n)
                        upto(pool, s_acc2, n - 1)
                        upto(pool, s_acc1, n - 1)
                        pool.tensor_tensor(x1sq[:, :, :], x1[d][:, :, :], x1[d][:, :, :], ALU.mult).then_inc(s_sq, 1)
                        a = acc_x[:, TPC * d:TPC * (d + 1), :]
                        pool.tensor_tensor(a, a, x1[d][:, :, :], ALU.add).then_inc(s_acc1, 1)
                        pool.wait_ge(s_sq, n)
                        a = acc_x2[:, TPC * d:TPC * (d + 1), :]
                        pool.tensor_tensor(a, a, x1sq[:, :, :], ALU.add).then_inc(s_acc2, 1)

                slots(pool, slot)

            @block.vector
            def _(dve):
                fold = [0]

                def link(ins):
                    fold[0] += 1
                    ins.then_inc(s_fold, 1)
                    dve.wait_ge(s_fold, fold[0])

                dve.wait_ge(s_w, 16 * 11)
                for h in range(2):
                    dve.tensor_scalar(wBs[:, h, :], wB[:, h, :], l1[:, h, 0:1], None, ALU.mult)
                    last = dve.tensor_scalar(w1s[:, h, :], w1[:, h, :], l2[:, h, 0:1], None, ALU.mult)
                link(last)
                for k in range(NT):
                    dve.wait_ge(s_xs[k % 2], 16 * (k // 2 + 1))
                    for g in range(GROUPS):
                        last = dve.bn_stats(st[:, GROUPS * k + g, :], xs[k % 2][:, :, CG * g:CG * (g + 1)])
                    last.then_inc(s_bn, 1)
                dve.wait_ge(s_bn, NT)
                per = T * CG / 2
                link(dve.tensor_tensor(pm[:, 0, :], st[:, :, 1], st[:, :, 4], ALU.add))
                link(dve.tensor_tensor(sq[:, 0, :], st[:, :, 1], st[:, :, 1], ALU.mult))
                link(dve.tensor_tensor(sq[:, 1, :], st[:, :, 4], st[:, :, 4], ALU.mult))
                link(dve.tensor_tensor(sq[:, 0, :], sq[:, 0, :], sq[:, 1, :], ALU.add))
                link(dve.tensor_tensor(sq[:, 1, :], st[:, :, 2], st[:, :, 5], ALU.add))
                link(dve.scalar_tensor_tensor(out=pm[:, 1, :], in0=sq[:, 1, :], scalar=1.0 / per,
                                              in1=sq[:, 0, :], op0=ALU.mult, op1=ALU.add))
                dve.wait_ge(s_sum, 1)
                dve.tensor_copy(hbias[:, :], ps_g[0:HALF, 0, 0:2])
                link(dve.tensor_tensor(b1f[:, :], ps_g[:, 0, 8:8 + FT], b1c[:, :], ALU.add))
                dve.wait_ge(s_sum, 2)
                link(dve.tensor_scalar(gmean[:, :], ps_h[:, 0, 0:256], 0.5, None, ALU.mult))
                link(dve.tensor_tensor(gshift[:, :], gmean[:, :], gmean[:, :], ALU.mult))
                dve.scalar_tensor_tensor(out=gvar[:, :], in0=ps_h[:, 0, 256:512], scalar=0.5,
                                         in1=gshift[:, :], op0=ALU.mult, op1=ALU.subtract).then_inc(s_tab, 1)
                dve.wait_ge(s_tab, 1)
                link(dve.tensor_scalar(gvar[:, :], gvar[:, :], GN_EPS, None, ALU.add))
                dve.wait_ge(s_pow, 1)
                link(dve.tensor_tensor(gshift[:, :], gmean[:, :], grstd[:, :], ALU.mult))
                for tab, src in ((R1, grstd), (M1, gshift)):
                    last = dve.tensor_copy(tab[:, :, :].rearrange("p k (g e) -> p (k g) e", e=CG),
                                           src[:, :].unsqueeze(2).to_broadcast([P, NT * GROUPS, CG]))
                link(last)

                def slot(t, c):
                    n = CHUNKS * t + c
                    if there(n - 1):
                        d = 1 - c
                        dve.wait_ge(s_w2, n)
                        if not isinstance(n, int) or n >= 3:
                            dve.wait_ge(s_acc2, n - 2)
                            dve.wait_ge(s_st[d], STORES * (t if c else t - 1))
                        dve.tensor_tensor(two(x1[d]), tok(ps_o), two(res[d]), ALU.add).then_inc(s_x1, 1)
                    if there(n + 2):
                        dve.wait_ge(s_x[c], 16 * (t + 2))
                        upto(dve, s_t1, n + 1)
                        r = slice(TPC * c, TPC * (c + 1))
                        dve.tensor_tensor(xn[c][:, :, :], xt[c][:, :, :], R1[:, r, :], ALU.mult).then_inc(s_gs, 1)
                        dve.wait_ge(s_gs, n + 3)
                        dve.tensor_tensor(xn[c][:, :, :], xn[c][:, :, :], M1[:, r, :],
                                          ALU.subtract).then_inc(s_gn, 1)
                        dve.wait_ge(s_gn, n + 3)
                        for k in range(TPC):
                            last = dve.bn_stats(s6a[:, k, :], xn[c][:, k, :])
                        last.then_inc(s_st1, 1)
                        dve.wait_ge(s_w, 16 * 11)
                        dve.wait_ge(s_st1, n + 3)
                        for k in range(TPC):
                            last = dve.bn_aggr(mva[:, k, :], s6a[:, k, :])
                        last.then_inc(s_ag1, 1)
                        dve.wait_ge(s_ag1, n + 3)
                        dve.tensor_scalar(vea[:, :], mva[:, :, 1], LN_EPS, None, ALU.add).then_inc(s_ve1, 1)
                        dve.wait_ge(s_rs1, n + 3)
                        for k in range(TPC):
                            last = dve.tensor_scalar(xn[c][:, k, :], xn[c][:, k, :], mva[:, k, 0:1], rsa[:, k:k + 1],
                                                     ALU.subtract, ALU.mult)
                        last.then_inc(s_xn, 1)
                    if there(n + 1):
                        d = 1 - c
                        dve.wait_ge(s_cm, n + 2)
                        for k in range(TPC):
                            last = dve.bn_stats(s6b[:, k, :], tok_tile(ps_r, k))
                        last.then_inc(s_st2, 1)
                        dve.wait_ge(s_w, 16 * 11)
                        dve.wait_ge(s_st2, n + 2)
                        for k in range(TPC):
                            last = dve.bn_aggr(mvb[:, k, :], s6b[:, k, :])
                        last.then_inc(s_ag2, 1)
                        dve.wait_ge(s_ag2, n + 2)
                        dve.tensor_scalar(veb[:, :], mvb[:, :, 1], LN_EPS, None, ALU.add).then_inc(s_ve2, 1)
                        dve.wait_ge(s_res, n + 2)
                        dve.tensor_tensor(two(res[d]), tok(ps_r), two(res[d]), ALU.add).then_inc(s_rsum, 1)
                        dve.wait_ge(s_rs2, n + 2)
                        upto(dve, s_t2, n + 1)
                        for k in range(TPC):
                            last = dve.tensor_scalar(yb[:, k, :], tok_tile(ps_r, k), mvb[:, k, 0:1], rsb[:, k:k + 1],
                                                     ALU.subtract, ALU.mult)
                        last.then_inc(s_y, 1)

                slots(dve, slot)

            @block.tensor
            def _(pe):
                pe.wait_ge(s_w, 16 * 11)
                for m in range(2):
                    for h in range(2):
                        pe.matmul(ps_g[0:HALF, 0, m:m + 1], wB[:, h, HALF * m:HALF * (m + 1)], l1[:, h, 1:2],
                                  start=(h == 0), stop=(h == 1))
                for f in range(FT):
                    for h in range(2):
                        last = pe.matmul(ps_g[:, 0, 8 + f:9 + f], w1[:, h, P * f:P * (f + 1)], l2[:, h, 1:2],
                                         start=(h == 0), stop=(h == 1))
                last.then_inc(s_sum, 1)
                pe.wait_ge(s_fold, 7)
                pe.matmul(ps_h[:, 0, :], blockm[:, :], pm[:, :, :].rearrange("p a g -> p (a g)"),
                          start=True, stop=True).then_inc(s_sum, 1)
                pe.wait_ge(s_fold, 12)
                pe.wait_ge(s_init, 1)

                def transposes(dst, src):
                    for h in range(2):
                        for k in range(TPC):
                            last = pe.transpose(dst[0:HALF, h, P * k:P * (k + 1)],
                                                src[:, k, HALF * h:HALF * (h + 1)], ident[:, :])
                    return last

                def slot(t, c):
                    n = CHUNKS * t + c
                    if there(n + 1):
                        d = 1 - c
                        pe.wait_ge(s_xnT, n + 2)
                        if not isinstance(n, int) or n >= 1:
                            pe.wait_ge(s_h, n)
                        for m in range(2):
                            cols = slice(HALF * m, HALF * (m + 1))
                            for h in range(2):
                                pe.matmul(ps_h[0:HALF, m, :], wBs[:, h, cols], xnT[d][:, h, :],
                                          start=(h == 0), stop=False)
                            for h in range(2):
                                last = pe.matmul(ps_h[0:HALF, m, :], wA[:, h, cols], hT[d][:, h, :],
                                                 start=False, stop=(h == 1))
                        last.then_inc(s_scan, 1)
                    if there(n):
                        pe.wait_ge(s_yT, n + 1)
                        for f in range(FT):
                            if f >= 2:
                                pe.wait_ge(s_gelu, FT * n + f - 1)
                            for h in range(2):
                                last = pe.matmul(ps_g[:, f % 2, :], w1s[:, h, P * f:P * (f + 1)], yT[:, h, :],
                                                 start=(h == 0), stop=(h == 1))
                            last.then_inc(s_w1, 1)
                    if there(n + 1):
                        d = 1 - c
                        pe.wait_ge(s_h, n + 2)
                        upto(pe, s_y, n + 1)
                        upto(pe, s_rsum, n + 1)
                        for k in range(TPC):
                            for h in range(2):
                                last = pe.matmul(tok_tile(ps_r, k), hT[d][:, h, P * k:P * (k + 1)], wC[:, h, :],
                                                 start=(h == 0), stop=(h == 1))
                        last.then_inc(s_cm, 1)
                    if there(n + 2):
                        pe.wait_ge(s_xn, n + 3)
                        upto(pe, s_h, n + 2)
                        transposes(ps_h, xn[c]).then_inc(s_t1, 1)
                    if there(n):
                        upto(pe, s_x1, n)
                        for f in range(0, FT, FT - 1):
                            pe.wait_ge(s_gelu, FT * n + f + 1)
                        for k in range(TPC):
                            for f in range(FT):
                                last = pe.matmul(tok_tile(ps_o, k), gT[:, f, P * k:P * (k + 1)], w2[:, f, :],
                                                 start=(f == 0), stop=(f == FT - 1))
                        last.then_inc(s_w2, 1)
                    if there(n + 1):
                        pe.wait_ge(s_y, n + 2)
                        if isinstance(n, int) and n < 0:
                            pass
                        else:
                            pe.wait_ge(s_gelu, FT * n + FT)
                        transposes(ps_g, yb).then_inc(s_t2, 1)

                slots(pe, slot)


        bias_tab = [[top.enter_context(nc.sbuf_tensor(f"bias_{r}{k}", [P, HEADS, T], fp32)) for k in range(2)]
                    for r in range(2)]
        with ExitStack() as ctx:
            def sb(name, shape):
                return ctx.enter_context(nc.sbuf_tensor(name, shape, fp32))

            def ps(name, shape):
                return ctx.enter_context(nc.psum_tensor(name, shape, fp32))

            NG = NT * GROUPS
            RPB = (2 * WS - 1) ** 2
            hot0, hot1 = sb("hot0", [P, T, P]), sb("hot1", [RPB - P, T, P])
            tab0, tab1 = sb("tab0", [P, HEADS]), sb("tab1", [RPB - P, HEADS])
            mask = sb("mask", [P, 4, T])
            pm2 = sb("pm2", [P, 2, NG])
            mean2, var2, rstd2, shift2 = (sb(f"{w}2", [P, NG]) for w in ("mean", "var", "rstd", "shift"))
            scale_ch, shift_ch = sb("scale_ch", [P, NT, C]), sb("shift_ch", [P, NT, C])
            gcol = sb("gcol", [HALF, IMGS, 4])
            ps_m = ps("ps_m", [P, 512])
            ps_c = ps("ps_c", [P, IMGS, 2, 2])
            ps_b = ps("ps_b", [P, 2, 512])
            MB = 512 // HEADS
            s_l = sem("tables_loaded")
            s_v2, s_p2, s_m2, s_s2 = sem("gn2_steps"), sem("gn2_rstd"), sem("gn2_sums"), sem("gn2_stored")
            s_b2 = sem("bias_gathered")
            block = ctx.enter_context(nc.Block())

            @block.sync
            def _(sp):
                for dst, src in ((hot0[:, :, :], onehot[0:P]), (hot1[:, :, :], onehot[P:RPB]),
                                 (tab0[:, :], rpb[0:P]), (tab1[:, :], rpb[P:RPB]), (mask[:, :, :], shift_mask)):
                    sp.dma_start(dst, src).then_inc(s_l, 16)
                sp.wait_ge(s_v2, 9)
                for r in range(CELLS):
                    sp.dma_start(gn2_cols[r].rearrange("i p s -> p i s"), gcol[:, :, :]).then_inc(s_s2, 16)
                sp.wait_ge(s_s2, 16 * CELLS)

            @block.gpsimd
            def _(pool):
                pool.wait_ge(s_v2, 5)
                pool.tensor_tensor(rstd2[:, :], var2[:, :], neg_half[:, :], ALU.pow).then_inc(s_p2, 1)

            @block.tensor
            def _(pe):
                pe.wait_ge(s_v2, 1)
                pe.matmul(ps_m[:, :], blockm[:, :], pm2[:, :, :].rearrange("p a g -> p (a g)"),
                          start=True, stop=True).then_inc(s_m2, 1)
                pe.wait_ge(s_l, 16 * 5)
                for m in range(T):
                    dst = ps_b[:, m // MB, (m % MB) * HEADS:(m % MB + 1) * HEADS]
                    pe.matmul(dst, hot0[:, m, :], tab0[:, :], start=True, stop=False)
                    last = pe.matmul(dst, hot1[:, m, :], tab1[:, :], start=False, stop=True)
                last.then_inc(s_b2, 1)
                pe.wait_ge(s_v2, 8)
                for k in range(NT):
                    for a, tab in enumerate((scale_ch, shift_ch)):
                        for h in range(2):
                            last = pe.matmul(ps_c[0:HALF, 2 * k:2 * k + 2, a, h], tab[:, k, HALF * h:HALF * (h + 1)],
                                             ident[:, 0:WINS + 1:WINS], start=True, stop=True)
                last.then_inc(s_m2, 1)

            @block.vector
            def _(dve):
                done = [0]

                def link(ins):
                    done[0] += 1
                    ins.then_inc(s_v2, 1)
                    dve.wait_ge(s_v2, done[0])

                for k, acc in enumerate((acc_x, acc_x2)):
                    last = dve.tensor_reduce(pm2[:, k, :], acc[:, :, :].rearrange("p k (g e) -> p (k g) e", e=CG),
                                             AX.X, ALU.add)
                link(last)
                dve.wait_ge(s_m2, 1)
                per = 1.0 / (T * CG)
                link(dve.tensor_scalar(mean2[:, :], ps_m[:, 0:NG], per, None, ALU.mult))
                link(dve.tensor_tensor(shift2[:, :], mean2[:, :], mean2[:, :], ALU.mult))
                link(dve.scalar_tensor_tensor(out=var2[:, :], in0=ps_m[:, NG:2 * NG], scalar=per,
                                              in1=shift2[:, :], op0=ALU.mult, op1=ALU.subtract))
                link(dve.tensor_scalar(var2[:, :], var2[:, :], GN_EPS, None, ALU.add))
                dve.wait_ge(s_p2, 1)
                link(dve.tensor_tensor(shift2[:, :], mean2[:, :], rstd2[:, :], ALU.mult))
                link(dve.tensor_scalar(shift2[:, :], shift2[:, :], -1.0, None, ALU.mult))
                for tab, src in ((scale_ch, rstd2), (shift_ch, shift2)):
                    last = dve.tensor_copy(tab[:, :, :].rearrange("p k (g e) -> p (k g) e", e=CG),
                                           src[:, :].unsqueeze(2).to_broadcast([P, NG, CG]))
                link(last)
                dve.wait_ge(s_m2, 2)
                link(dve.tensor_copy(gcol[:, :, :], ps_c[0:HALF].rearrange("p i a h -> p i (a h)")))
                dve.wait_ge(s_b2, 1)
                for r in range(2):
                    for k in range(2):
                        for b in range(2):
                            m0, m1 = MB * b, min(MB * (b + 1), T)
                            src = ps_b[:, b, 0:(m1 - m0) * HEADS].rearrange("p (m h) -> p h m", h=HEADS)
                            msk = mask[:, 2 * r + k, m0:m1].unsqueeze(1).to_broadcast([P, HEADS, m1 - m0])
                            last = dve.tensor_tensor(bias_tab[r][k][:, :, m0:m1], src, msk, ALU.add)
                link(last)

        with ExitStack() as ctx:
            def sb(name, shape):
                return ctx.enter_context(nc.sbuf_tensor(name, shape, fp32))

            def ps(name, shape):
                return ctx.enter_context(nc.psum_tensor(name, shape, fp32))

            UW = UP * P
            NW = 2 * UP
            JP = 2 * PAIRS
            wqkv = sb("wqkv", [HALF, 2, 3 * C])
            wp = sb("wp", [HALF, 2, C])
            bqkv = sb("bqkv", [HALF, 3, 2])
            hm = sb("hm", [HALF, 5])
            bqm, bkm = sb("bqm", [HALF, 2, PAIRS]), sb("bkm", [HALF, 2, 2])
            pbb = sb("pbb", [P, C])
            xb = [sb(f"xb{b}", [P, UP, C]) for b in range(2)]
            gnc = [sb(f"gnc{b}", [HALF, 2, 2]) for b in range(2)]
            rs = [sb(f"rs{b}", [P, UP, C]) for b in range(2)]
            yo = [sb(f"yo{b}", [P, UP, C]) for b in range(2)]
            xT = sb("xT", [HALF, 2, UW])
            Qm = [sb(f"Qm{b}", [HALF, 2, PAIRS, NW, SLOT]) for b in range(2)]
            Kp = [sb(f"Kp{b}", [HALF, 2, 2, NW, T]) for b in range(2)]
            Vx = [sb(f"Vx{b}", [P, NW, JP, 2 * HD]) for b in range(2)]
            L = [sb(f"L{b}", [P, HEADS, T]) for b in range(UP)]
            E = [sb(f"E{b}", [P, HEADS, SLOT]) for b in range(UP)]
            mx = [sb(f"mx{b}", [P, HEADS]) for b in range(UP)]
            sm = [sb(f"sm{b}", [P, HEADS]) for b in range(UP)]
            ri = [sb(f"ri{b}", [P, HEADS]) for b in range(UP)]
            PT = [sb(f"PT{b}", [P, JP, P]) for b in range(2)]
            oT = [[sb(f"oT{b}{p}", [HALF, 2, 2, SLOT]) for p in range(UP)] for b in range(2)]
            ps_s = [ps(f"ps_s{b}", [P, 2, 512]) for b in range(2)]
            ps_t = ps("ps_t", [P, 2, 512])
            ps_v = ps("ps_v", [P, 512])
            ps_w = ps("ps_w", [P, 512])

            s_w3, s_i3 = sem("attention_weights_loaded"), sem("attention_init")
            s_pad = sem("attention_pads_set")
            s_xb = [sem(f"unit_loaded{b}") for b in range(2)]
            s_tx, s_xT = sem("unit_transposed"), sem("unit_normed")
            s_q, s_qm = sem("q_summed"), sem("q_masked")
            s_k, s_kp = sem("k_summed"), sem("k_masked")
            s_v, s_vx = sem("v_summed"), sem("v_spread")
            s_sc, s_lg, s_mx, s_sub = sem("scores_summed"), sem("logits"), sem("row_maxima"), sem("maxima_off")
            s_ex, s_sm, s_ri, s_nm = sem("exponentials"), sem("row_sums"), sem("row_reciprocals"), sem("probabilities")
            s_pt, s_ptc = sem("probs_transposed"), sem("probs_copied")
            s_pv, s_o = sem("values_summed"), sem("heads_ready")
            s_pj, s_yo = sem("projected"), sem("unit_out_ready")
            s_rs = sem("unit_residual")
            s_so = [sem(f"unit_stored{b}") for b in range(2)]
            LOADS = 2 + 1
            block = ctx.enter_context(nc.Block())

            def units(engine, slot):
                last_row = IMGS * (CELLS - 1)
                for u in range(-1, 4):
                    slot(u // 2, u % 2, 0)
                with engine.Fori(2, last_row // 2) as i:
                    slot(i, 0, 0)
                    slot(i, 1, 0)
                with engine.Fori(last_row // 2, UNITS // 2 - 1) as i:
                    slot(i, 0, 1)
                    slot(i, 1, 1)
                for u in (UNITS - 2, UNITS - 1, UNITS):
                    slot(u // 2, u % 2, 1)

            def is_unit(u):
                return not isinstance(u, int) or 0 <= u < UNITS

            def lagged(u, c, p):
                return (u, c, p - 2) if p >= 2 else (u - 1, 1 - c, p + 2)

            @block.sync
            def _(sp):
                for dst, src in ((wqkv[:, :, :], qkvT.rearrange("(h p) n -> p h n", h=2)),
                                 (wp[:, :, :], projT.rearrange("(h p) n -> p h n", h=2)),
                                 (bqkv[:, :, :], qkv_b),
                                 (hm[:, :], head_masks), (pbb[:, :], proj_b.partition_broadcast(P))):
                    sp.dma_start(dst, src).then_inc(s_w3, 16)
                sp.wait_ge(s_pad, 1)

                x1_rows = x1_cells.rearrange("r k w t c -> (r k) w t c")
                cols = gn2_cols.rearrange("r k p s -> (r k) p s")

                def load(i, c):
                    u = 2 * i + c
                    for w in range(2):
                        src = x1_rows[bass.ds(u + IMGS, 1), w + 1:w + 2 * UP:2, :, :].rearrange("u w t c -> (u t) w c")
                        sp.dma_start(xb[c][SLOT * w:SLOT * w + T, :, :], src).then_inc(s_xb[c], 16)
                    sp.dma_start(gnc[c][:, :, :].rearrange("p s h -> p (s h)"),
                                 cols[bass.ds(u, 1), :, :].rearrange("u p s -> (u p) s"))\
                      .then_inc(s_xb[c], 16)

                def slot(i, c, r):
                    u = 2 * i + c
                    if is_unit(u + 2):
                        upto(sp, s_rs, u + 1)
                        upto(sp, s_xT, 2 * u + 2)
                        load(i + 1, c)
                    if is_unit(u - 1):
                        d = 1 - c
                        sp.wait_ge(s_yo, 2 * u)
                        for w in range(2):
                            src = yo[d][SLOT * w:SLOT * w + T, :, :]
                            sp.dma_start(out[bass.ds(u - 1, 1), :, w, :, :].rearrange("u p t c -> (u t) p c"), src)\
                              .then_inc(s_so[d], 16)

                load(0, 0)
                units(sp, slot)
                for d in range(2):
                    sp.wait_ge(s_so[d], 32 * UNITS // 2)

            @block.gpsimd
            def _(pool):
                for b in range(2):
                    pool.memset(xb[b][:, :, :], 0.0)
                    pool.memset(Qm[b][:, :, :, :, :], 0.0)
                    for p in range(UP):
                        pool.memset(oT[b][p][:, :, :, :], 0.0)
                pool.memset(rs[0][:, :, :], 0.0).then_inc(s_pad, 1)
                pool.wait_ge(s_w3, 16 * 5)

                def norm(u, p):
                    k = UP * u + p
                    pool.wait_ge(s_ri, k + 1)
                    e = E[p][:, :, 0:T]
                    pool.tensor_tensor(e, e, ri[p][:, :].unsqueeze(2).to_broadcast([P, HEADS, T]), ALU.mult)\
                        .then_inc(s_nm, 1)

                def slot(i, c, r):
                    u = 2 * i + c
                    for p in range(UP):
                        pu, pp = (u, p - 1) if p else (u - 1, UP - 1)
                        if is_unit(pu):
                            norm(pu, pp)
                    if is_unit(u + 1):
                        d = 1 - c
                        pool.wait_ge(s_xb[d], 16 * LOADS * (i + 1 if c == 0 else i + 2))
                        upto(pool, s_yo, 2 * u)
                        pool.tensor_tensor(rs[d][:, :, :], xb[d][:, :, :],
                                           pbb[:, :].unsqueeze(1).to_broadcast([P, UP, C]), ALU.add)\
                            .then_inc(s_rs, 1)

                units(pool, slot)

            @block.scalar
            def _(act):
                act.wait_ge(s_w3, 16 * 5)
                act.wait_ge(s_i3, 2)
                act.wait_ge(s_pad, 1)

                def normed(i, c, h):
                    v, d = 2 * i + c + 1, 1 - c
                    act.wait_ge(s_tx, 2 * v + h + 1)
                    if h == 0:
                        upto(act, s_v, 2 * v)
                    act.activation(xT[:, h, :], ps_w[0:HALF, :], ACT.Identity,
                                   scale=gnc[d][:, 0, h:h + 1], bias=gnc[d][:, 1, h:h + 1]).then_inc(s_xT, 1)

                def query(i, c, h):
                    v, d = 2 * i + c + 1, 1 - c
                    act.wait_ge(s_q, 2 * v + h + 1)
                    if h == 0:
                        upto(act, s_sc, UP * (v - 1))
                    for j in range(PAIRS):
                        last = act.activation(Qm[d][:, h, j, :, 0:T],
                                              ps_w[0:HALF, 0:NW * T].rearrange("p (w t) -> p w t", t=T),
                                              ACT.Identity, scale=hm[:, j:j + 1], bias=bqm[:, h, j:j + 1])
                    last.then_inc(s_qm, 1)

                def key(i, c, h):
                    v, d = 2 * i + c + 1, 1 - c
                    act.wait_ge(s_k, 2 * v + h + 1)
                    for e in range(2):
                        last = act.activation(Kp[d][:, h, e, :, :],
                                              ps_w[0:HALF, 0:NW * T].rearrange("p (w t) -> p w t", t=T),
                                              ACT.Identity, scale=hm[:, PAIRS + e:PAIRS + e + 1],
                                              bias=bkm[:, h, e:e + 1])
                    last.then_inc(s_kp, 1)

                def slot(i, c, r):
                    u = 2 * i + c
                    nxt = is_unit(u + 1)
                    for p in range(UP):
                        lu, lc, lp = lagged(u, c, p)
                        k = UP * u + p - 2
                        if nxt and p == 0:
                            normed(i, c, 0)
                        if nxt and p == 1:
                            query(i, c, 1)
                        if is_unit(lu):
                            act.wait_ge(s_pt, k + 1)
                            upto(act, s_pv, k - 1)
                            act.activation(PT[lp % 2][:, :, :].rearrange("p (a b) q -> p a (b q)", a=2),
                                           ps_t[:, :, 0:PAIRS * P], ACT.Copy).then_inc(s_ptc, 1)
                        if nxt and p == 0:
                            normed(i, c, 1)
                        if nxt and p == 1:
                            key(i, c, 0)
                        if is_unit(lu):
                            act.wait_ge(s_pv, k + 1)
                            upto(act, s_pj, 2 * (lu - 1))
                            for h in range(2):
                                src = ps_v[0:HALF, h * P:(h + 1) * P].rearrange("p (w t) -> p w t", w=2)
                                last = act.activation(oT[lc][lp][:, h, :, 0:T], src[:, :, 0:T], ACT.Identity,
                                                      bias=bqkv[:, 2, h:h + 1])
                            last.then_inc(s_o, 1)
                        if nxt and p == 0:
                            query(i, c, 0)
                        if nxt and p == 1:
                            key(i, c, 1)
                        if is_unit(u):
                            k = UP * u + p
                            act.wait_ge(s_sub, k + 1)
                            upto(act, s_pt, k - 3)
                            act.activation(E[p][:, :, 0:T], L[p][:, :, :], ACT.Exp).then_inc(s_ex, 1)

                units(act, slot)

            @block.vector
            def _(dve):
                for b in range(2):
                    dve.memset(Vx[b][:, :, :, :], 0.0)
                for p in range(UP):
                    last = dve.memset(E[p][:, :, :], 0.0)
                last.then_inc(s_i3, 1)
                dve.wait_ge(s_w3, 16 * 5)
                for h in range(2):
                    dve.tensor_scalar(bqm[:, h, :], hm[:, 0:PAIRS], bqkv[:, 0, h:h + 1], None, ALU.mult)
                    last = dve.tensor_scalar(bkm[:, h, :], hm[:, PAIRS:PAIRS + 2], bqkv[:, 1, h:h + 1], None, ALU.mult)
                last.then_inc(s_i3, 1)
                dve.wait_ge(s_i3, 2)

                def spread(i, c, half):
                    v, d = 2 * i + c + 1, 1 - c
                    dve.wait_ge(s_v, 2 * v + half + 1)
                    if half == 0:
                        upto(dve, s_pv, UP * (v - 1))
                    for w in range(2):
                        for e in range(2):
                            src = ps_w[SLOT * w:SLOT * (w + 1), 0:2 * C]\
                                .rearrange("p (a j e) -> p a j e", a=2, j=JP)[:, :, :, HD * e:HD * (e + 1)]
                            last = dve.tensor_copy(
                                Vx[d][SLOT * e:SLOT * (e + 1), 4 * half + w:4 * half + w + 3:2, :, HD * e:HD * (e + 1)],
                                src)
                    last.then_inc(s_vx, 1)

                def finish(i, c, half):
                    v, d = 2 * i + c - 1, 1 - c
                    dve.wait_ge(s_pj, 2 * v + half + 1)
                    if half == 0:
                        dve.wait_ge(s_rs, v + 1)
                        upto(dve, s_so[d], 32 * (i if c else i - 1))
                    ab = slice(2 * half, 2 * half + 2)
                    dve.tensor_tensor(yo[d][:, ab, :], ps_w[:, 0:2 * C].rearrange("p (a c) -> p a c", a=2),
                                      rs[d][:, ab, :], ALU.add).then_inc(s_yo, 1)

                def slot(i, c, r):
                    u = 2 * i + c
                    nxt = is_unit(u + 1)
                    for p in range(UP):
                        pu, pp = (u, p - 1) if p else (u - 1, UP - 1)
                        if is_unit(pu):
                            k = UP * u + p - 1
                            dve.wait_ge(s_ex, k + 1)
                            dve.tensor_reduce(sm[pp][:, :], E[pp][:, :, 0:T], AX.X, ALU.add).then_inc(s_sm, 1)
                            dve.wait_ge(s_sm, k + 1)
                            dve.reciprocal(ri[pp][:, :], sm[pp][:, :]).then_inc(s_ri, 1)
                        if is_unit(u):
                            k = UP * u + p
                            dve.wait_ge(s_sc, k + 1)
                            tab = bias_tab[r][p // (UP - 1)][:, :, :].rearrange("p (a h) m -> p a (h m)", a=2)
                            dve.scalar_tensor_tensor(out=L[p][:, :, :].rearrange("p (a h) m -> p a (h m)", a=2),
                                                     in0=ps_s[p % 2][:, :, 0:HEADS // 2 * T], scalar=HD ** -0.5,
                                                     in1=tab, op0=ALU.mult, op1=ALU.add).then_inc(s_lg, 1)
                        if nxt and p == 2:
                            spread(i, c, 0)
                        if is_unit(u):
                            dve.wait_ge(s_lg, k + 1)
                            dve.tensor_reduce(mx[p][:, :], L[p][:, :, :], AX.X, ALU.max).then_inc(s_mx, 1)
                            dve.wait_ge(s_mx, k + 1)
                            dve.tensor_tensor(L[p][:, :, :], L[p][:, :, :],
                                              mx[p][:, :].unsqueeze(2).to_broadcast([P, HEADS, T]),
                                              ALU.subtract).then_inc(s_sub, 1)
                        if nxt and p == 2:
                            spread(i, c, 1)
                        if is_unit(u - 1) and p >= 2:
                            finish(i, c, p - 2)

                units(dve, slot)

            @block.tensor
            def _(pe):
                pe.wait_ge(s_w3, 16 * 5)
                pe.wait_ge(s_i3, 2)
                pe.wait_ge(s_pad, 1)

                def turn(i, c, h):
                    v, d = 2 * i + c + 1, 1 - c
                    if h == 0:
                        pe.wait_ge(s_xb[d], 16 * LOADS * (i + 1 if c == 0 else i + 2))
                        if isinstance(v, int) and v <= 2:
                            upto(pe, s_vx, 2 * v)
                        else:
                            pe.wait_ge(s_yo, 2 * (v - 2))
                    else:
                        pe.wait_ge(s_xT, 2 * v + 1)
                    for p in range(UP):
                        last = pe.transpose(ps_w[0:HALF, P * p:P * (p + 1)],
                                            xb[d][:, p, HALF * h:HALF * (h + 1)], ident[:, :])
                    last.then_inc(s_tx, 1)

                def project(i, c, h, part, free, count, done):
                    pe.wait_ge(free, count)
                    for k in range(2):
                        last = pe.matmul(ps_w[0:HALF, 0:NW * T].rearrange("p (w t) -> p w t", t=T),
                                         wqkv[:, k, C * part + HALF * h:C * part + HALF * (h + 1)],
                                         xT[:, k, :].rearrange("p (w t) -> p w t", t=SLOT)[:, :, 0:T],
                                         start=(k == 0), stop=(k == 1))
                    last.then_inc(done, 1)

                def values(i, c, half):
                    v = 2 * i + c + 1
                    if half == 0:
                        pe.wait_ge(s_kp, 2 * v + 2)
                    else:
                        pe.wait_ge(s_vx, 2 * v + 1)
                    for a in range(2):
                        p = 2 * half + a
                        for k in range(2):
                            last = pe.matmul(ps_w[:, C * a:C * (a + 1)], xT[:, k, P * p:P * (p + 1)],
                                             wqkv[:, k, 2 * C:3 * C], start=(k == 0), stop=(k == 1))
                    last.then_inc(s_v, 1)

                def mix(i, c, half):
                    v, d = 2 * i + c - 1, 1 - c
                    pe.wait_ge(s_o, UP * v + 2 * half + 2)
                    if half == 1:
                        pe.wait_ge(s_yo, 2 * v + 1)
                    elif is_unit(v + 2):
                        pe.wait_ge(s_vx, 2 * v + 6)
                    for a in range(2):
                        p = 2 * half + a
                        for k in range(2):
                            last = pe.matmul(ps_w[:, C * a:C * (a + 1)],
                                             oT[d][p][:, k, :, :].rearrange("p w t -> p (w t)"),
                                             wp[:, k, :], start=(k == 0), stop=(k == 1))
                    last.then_inc(s_pj, 1)

                def slot(i, c, r):
                    u = 2 * i + c
                    v = u + 1
                    nxt = is_unit(v)
                    for p in range(UP):
                        lu, lc, lp = lagged(u, c, p)
                        if is_unit(u):
                            k = UP * u + p
                            if p == 0:
                                pe.wait_ge(s_qm, 2 * u + 2)
                                pe.wait_ge(s_kp, 2 * u + 2)
                            upto(pe, s_lg, k - 1)
                            for w in range(2):
                                for h in range(2):
                                    for j in range(PAIRS):
                                        last = pe.matmul(ps_s[p % 2][SLOT * w:SLOT * (w + 1), h, 2 * T * j:2 * T * (j + 1)],
                                                         Qm[c][:, h, j, 2 * p + w, :],
                                                         Kp[c][:, h, :, 2 * p + w, :], start=True, stop=True)
                            last.then_inc(s_sc, 1)
                        if nxt:
                            if p == 0:
                                turn(i, c, 0)
                            if p == 1:
                                project(i, c, 1, 0, s_qm, 2 * v + 1, s_q)
                            if p == 2:
                                values(i, c, 0)
                        if p == 3 and is_unit(u - 1):
                            mix(i, c, 1)
                        if is_unit(lu):
                            k = UP * u + p - 2
                            pe.wait_ge(s_nm, k + 1)
                            upto(pe, s_ptc, k)
                            for j in range(JP):
                                last = pe.transpose(ps_t[:, j // PAIRS, P * (j % PAIRS):P * (j % PAIRS + 1)],
                                                    E[lp][:, 2 * j:2 * j + 2, :].rearrange("p h m -> p (h m)"),
                                                    ident[:, :])
                            last.then_inc(s_pt, 1)
                        if nxt:
                            if p == 0:
                                turn(i, c, 1)
                            if p == 1:
                                project(i, c, 0, 1, s_qm, 2 * v + 2, s_k)
                            if p == 2:
                                values(i, c, 1)
                        if is_unit(lu):
                            pe.wait_ge(s_ptc, k + 1)
                            pe.wait_ge(s_vx, 2 * lu + 2)
                            upto(pe, s_o, k)
                            for w in range(2):
                                for h in range(2):
                                    for j in range(PAIRS):
                                        last = pe.matmul(
                                            ps_v[2 * HD * j:2 * HD * (j + 1), P * h + SLOT * w:P * h + SLOT * w + T],
                                            Vx[lc][:, 2 * lp + w, PAIRS * h + j, :],
                                            PT[lp % 2][:, PAIRS * h + j, SLOT * w:SLOT * w + T],
                                            start=True, stop=True)
                            last.then_inc(s_pv, 1)
                        if nxt:
                            if p == 0:
                                project(i, c, 0, 0, s_xT, 2 * v + 2, s_q)
                            if p == 1:
                                project(i, c, 1, 1, s_kp, 2 * v + 1, s_k)
                        if p == 2 and is_unit(u - 1):
                            mix(i, c, 0)

                units(pe, slot)



def by_window(a):
    a = np.asarray(a).reshape(NT, 2, CELLS, WS, CELLS, WS, C)
    return np.ascontiguousarray(a.transpose(0, 1, 2, 4, 3, 5, 6).reshape(NT, P, T, C))


def by_column(*vectors, rows):
    return np.ascontiguousarray(np.stack([np.asarray(v).reshape(-1, rows).T for v in vectors], 2))


def from_units(a):
    tok = np.array(cell_tokens())
    row = (WS * (np.arange(CELLS)[:, None] + tok[:, 0]) + tok[:, 2]) % SIDE
    col = (WS * (np.arange(CELLS)[:, None] + tok[:, 1]) + tok[:, 3]) % SIDE
    a = np.asarray(a).reshape(CELLS, IMGS, CELLS, T, C)
    y = np.empty((IMGS, SIDE, SIDE, C), a.dtype)
    y[np.arange(IMGS)[None, :, None, None], row[:, None, None, :], col[None, None, :, :]] = a
    return y


def shape_constants():
    f = np.float32
    part = np.arange(P)
    block_mean = ((part[:, None] // WINS) == (part[None, :] // WINS)).astype(f) / WINS
    ch = np.arange(HALF)
    masks = np.stack([(ch // (2 * HD) == j) for j in range(PAIRS)] + [(ch // HD % 2 == e) for e in range(2)], 1)
    tok = np.array(cell_tokens())
    yi = WS * tok[:, 0] + tok[:, 2] - SHIFT
    xi = WS * tok[:, 1] + tok[:, 3] - SHIFT
    rel = (yi[:, None] - yi[None, :] + WS - 1) * (2 * WS - 1) + xi[:, None] - xi[None, :] + WS - 1
    onehot = np.zeros(((2 * WS - 1) ** 2, T, P), f)
    for w in range(2):
        onehot[rel.T, np.arange(T)[:, None], SLOT * w + np.arange(T)[None, :]] = 1
    mask = np.zeros((P, 2, 2, T), f)
    for r in range(2):
        for k in range(2):
            for w in range(2):
                apart = np.zeros((T, T), bool)
                if r:
                    apart |= tok[:, None, 0] != tok[None, :, 0]
                if k and w:
                    apart |= tok[:, None, 1] != tok[None, :, 1]
                mask[SLOT * w:SLOT * w + T, r, k] = np.where(apart, -100.0, 0.0)
    return {"block_mean": block_mean, "identity": np.eye(P, dtype=f), "head_masks": masks.astype(f),
            "onehot": onehot, "shift_mask": mask.reshape(P, 4, T)}


def kernel(**inputs):
    import concourse.bacc as bacc
    from concourse.bass_utils import run_bass_kernel_spmd

    def plain(name):
        return np.ascontiguousarray(inputs[name])

    arrays = {"x": by_window(inputs["x"])}
    for name in ("A", "Bm", "Cm", "W1", "W2", "b2"):
        arrays[name] = plain("L0_conv_" + name)
    for name in ("ln1", "ln2"):
        arrays[name] = by_column(*(inputs[f"L0_conv_{name}_{k}"] for k in "wb"), rows=HALF)
    arrays["b1"] = by_column(inputs["L0_conv_b1"], rows=P)[:, :, 0]
    arrays["qkvT"] = np.ascontiguousarray(np.asarray(inputs["L1_conv_qkv_w"]).T)
    arrays["qkv_b"] = by_column(inputs["L1_conv_qkv_b"], rows=HALF)[:, :, 0].reshape(HALF, 3, 2)
    arrays["projT"] = np.ascontiguousarray(np.asarray(inputs["L1_conv_proj_w"]).T)
    arrays["proj_b"] = plain("L1_conv_proj_b")
    arrays["rpb"] = plain("L1_conv_rpb_table")
    arrays.update(shape_constants())
    nc = bacc.Bacc("TRN2", target_bir_lowering=False, num_devices=1)
    args = {n: nc.dram_tensor("in_" + n, a.shape, fp32, kind="ExternalInput").ap() for n, a in arrays.items()}
    out = nc.dram_tensor("out", (UNITS, UP, 2, T, C), fp32, kind="ExternalOutput").ap()
    build(nc, **args, out=out)
    r = run_bass_kernel_spmd(nc, [{"in_" + n: a for n, a in arrays.items()}], core_ids=[0])
    return from_units(r.results[0]["out"])
```

```python
from contextlib import ExitStack

import numpy as np

import concourse.bass as bass
from concourse import mybir

fp32 = mybir.dt.float32
f32r = mybir.dt.float32r
ALU = mybir.AluOpType
ACT = mybir.ActivationFunctionType
AX = mybir.AxisListType

IMGS, SIDE, C = 16, 56, 192
WS = 7
CELLS = SIDE // WS
WINS = CELLS * CELLS
T = WS * WS
SHIFT = 3
GROUPS, CG = 32, C // 32
HID = 4 * C
HEADS, HD = 12, 16
P = 128
CB = C - P
HALF = C // 2
PAIRS = HALF // (2 * HD)
NT = IMGS // 2
TPC = 4
CHUNKS = NT // TPC
NTOK = TPC * P
FT = HID // P
STEPS = T * CHUNKS
GN_EPS = LN_EPS = 1e-5
UNITS = CELLS * IMGS
SLOT = 64
UP = CELLS // 2
CROW = CELLS + 2


def cell_tokens():
    return [(int(i < SHIFT), int(j < SHIFT), i, j) for i in range(WS) for j in range(WS)]


def upto(engine, semaphore, count):
    if isinstance(count, int) and count <= 0:
        return
    engine.wait_ge(semaphore, count)


def build(nc, x, A, Bm, Cm, ln1, ln2, W1, b1, W2, b2,
          qkvT, qkv_b, projT, proj_b, rpb, block_mean, identity, head_masks, onehot, shift_mask, out):
    top = ExitStack()

    def sem(name):
        return top.enter_context(nc.semaphore(name))

    with top:
        x1_cells = nc.dram_tensor("x1_cells", [CROW, IMGS, CROW, T, C], fp32).ap()
        gn2_cols = nc.dram_tensor("gn2_cols", [CELLS, IMGS, HALF, 4], fp32).ap()

        def keep(name, shape):
            return top.enter_context(nc.sbuf_tensor(name, shape, fp32))

        ident = keep("ident", [P, P])
        blockm = keep("blockm", [P, P])
        neg_half = keep("neg_half", [P, 256])
        acc_x = keep("acc_x", [P, NT, C])
        acc_x2 = keep("acc_x2", [P, NT, C])

        class Split:

            def __init__(self, ctx, name, cols):
                self.parts = [ctx.enter_context(nc.sbuf_tensor(f"{name}_{k}", [P, cols], f32r))
                              for k in ("a_hi", "a_lo", "b_hi", "b_lo")]

            def terms(self, data_hi, data_lo, cols, pick=lambda t: t):
                a_hi, a_lo, b_hi, b_lo = (w[:, cols] for w in self.parts)
                da, db, dl = pick(data_hi[:, 0, :]), pick(data_hi[:, 1, :]), pick(data_lo[:, :])
                return (a_hi, da), (a_hi, dl), (a_lo, da), (b_hi, db), (b_lo, db)

        with ExitStack() as ctx:
            def sb(name, shape, dt=fp32, where=ctx):
                return where.enter_context(nc.sbuf_tensor(name, shape, dt))

            def ps(name, shape, where=ctx):
                return where.enter_context(nc.psum_tensor(name, shape, fp32))

            R1 = sb("R1", [P, NT, C])
            M1 = sb("M1", [P, NT, C])
            W_B, W_A, W_C = (Split(ctx, name, C) for name in ("wB", "wA", "wC"))
            W_1 = Split(ctx, "w1", HID)
            w2 = sb("w2", [P, FT, C])
            b2b = sb("b2b", [P, C])
            b1f = sb("b1f", [P, FT])
            hbias = sb("hbias", [P, 2])
            s_w = sem("weights_loaded")
            WEIGHT_LOADS = 11

            with ExitStack() as pre:
                xs = [sb(f"xs{b}", [P, T, C], where=pre) for b in range(2)]
                st = sb("st", [P, NT * GROUPS, 6], where=pre)
                pm = sb("pm", [P, 2, NT * GROUPS], where=pre)
                sq = sb("sq", [P, 2, NT * GROUPS], where=pre)
                gmean, gvar, grstd, gshift = (sb(f"g{w}", [P, NT * GROUPS], where=pre)
                                              for w in ("mean", "var", "rstd", "shift"))
                raw_B, raw_A, raw_C, fold_B = (sb(name, [P, 2, C], where=pre)
                                               for name in ("raw_B", "raw_A", "raw_C", "fold_B"))
                raw_1, fold_1 = sb("raw_1", [P, 2, HID], where=pre), sb("fold_1", [P, 2, HID], where=pre)
                l1, l2 = sb("l1", [P, 2, 2], where=pre), sb("l2", [P, 2, 2], where=pre)
                b1c = sb("b1c", [P, FT], where=pre)
                ps_g, ps_h = ps("ps_g0", [P, 512], where=pre), ps("ps_h0", [P, 512], where=pre)
                s_xs = [sem(f"stat_rows_loaded{b}") for b in range(2)]
                s_bn = sem("stat_rows_used")
                s_fold = sem("folded")
                s_sum = sem("group_sums")
                s_pow = sem("group_rstd")
                s_tab = sem("group_tables")
                s_i0 = sem("exponents_set")
                s_wh, s_wl = sem("weight_upper_parts"), sem("weight_lower_parts")
                block = pre.enter_context(nc.Block())

                @block.sync
                def _(sp):
                    for k in range(NT):
                        if k >= 2:
                            sp.wait_ge(s_bn, k - 1)
                        sp.dma_start(xs[k % 2][:, :, :], x[k]).then_inc(s_xs[k % 2], 16)

                @block.scalar
                def _(act):
                    for dst, src in ((ident[:, :], identity), (blockm[:, :], block_mean),
                                     (w2[:, :, :], W2.rearrange("(f p) n -> p f n", p=P)),
                                     (b2b[:, :], b2.partition_broadcast(P)),
                                     (l1[:, :, :], ln1), (l2[:, :, :], ln2), (b1c[:, :], b1)):
                        act.dma_start(dst, src).then_inc(s_w, 16)
                    for raw, src in ((raw_B, Bm), (raw_A, A), (raw_C, Cm), (raw_1, W1)):
                        act.dma_start(raw[:, :, :], src.rearrange("(k p) n -> p k n", p=P)).then_inc(s_w, 16)
                    act.wait_ge(s_fold, 1)
                    for full, parts in ((fold_B, W_B), (raw_A, W_A), (raw_C, W_C), (fold_1, W_1)):
                        for t in range(2):
                            last = act.activation(parts.parts[2 * t][:, :], full[:, t, :], ACT.Copy)
                    last.then_inc(s_wh, 1)

                @block.gpsimd
                def _(pool):
                    pool.memset(acc_x[:, :, :], 0.0)
                    pool.memset(acc_x2[:, :, :], 0.0)
                    pool.memset(neg_half[:, :], -0.5).then_inc(s_i0, 1)
                    pool.wait_ge(s_i0, 1)
                    pool.wait_ge(s_wh, 1)
                    for full, parts in ((fold_B, W_B), (raw_A, W_A), (raw_C, W_C), (fold_1, W_1)):
                        for t in range(2):
                            last = pool.tensor_tensor(parts.parts[2 * t + 1][:, :], full[:, t, :],
                                                      parts.parts[2 * t][:, :], ALU.subtract)
                    last.then_inc(s_wl, 1)
                    pool.wait_ge(s_fold, 11)
                    pool.tensor_tensor(grstd[:, :], gvar[:, :], neg_half[:, :], ALU.pow).then_inc(s_pow, 1)

                @block.vector
                def _(dve):
                    fold = [0]

                    def link(ins):
                        fold[0] += 1
                        ins.then_inc(s_fold, 1)
                        dve.wait_ge(s_fold, fold[0])

                    dve.wait_ge(s_w, 16 * WEIGHT_LOADS)
                    for t in range(2):
                        dve.tensor_scalar(fold_B[:, t, :], raw_B[:, t, :], l1[:, t, 0:1], None, ALU.mult)
                        last = dve.tensor_scalar(fold_1[:, t, :], raw_1[:, t, :], l2[:, t, 0:1], None, ALU.mult)
                    link(last)
                    for k in range(NT):
                        dve.wait_ge(s_xs[k % 2], 16 * (k // 2 + 1))
                        for g in range(GROUPS):
                            last = dve.bn_stats(st[:, GROUPS * k + g, :], xs[k % 2][:, :, CG * g:CG * (g + 1)])
                        last.then_inc(s_bn, 1)
                    dve.wait_ge(s_bn, NT)
                    per = T * CG / 2
                    link(dve.tensor_tensor(pm[:, 0, :], st[:, :, 1], st[:, :, 4], ALU.add))
                    link(dve.tensor_tensor(sq[:, 0, :], st[:, :, 1], st[:, :, 1], ALU.mult))
                    link(dve.tensor_tensor(sq[:, 1, :], st[:, :, 4], st[:, :, 4], ALU.mult))
                    link(dve.tensor_tensor(sq[:, 0, :], sq[:, 0, :], sq[:, 1, :], ALU.add))
                    link(dve.tensor_tensor(sq[:, 1, :], st[:, :, 2], st[:, :, 5], ALU.add))
                    link(dve.scalar_tensor_tensor(out=pm[:, 1, :], in0=sq[:, 1, :], scalar=1.0 / per,
                                                  in1=sq[:, 0, :], op0=ALU.mult, op1=ALU.add))
                    dve.wait_ge(s_sum, 1)
                    dve.tensor_copy(hbias[:, 0:1], ps_g[:, 0:1])
                    dve.tensor_copy(hbias[0:CB, 1:2], ps_g[0:CB, 1:2])
                    link(dve.tensor_tensor(b1f[:, :], ps_g[:, 8:8 + FT], b1c[:, :], ALU.add))
                    dve.wait_ge(s_sum, 2)
                    link(dve.tensor_scalar(gmean[:, :], ps_h[:, 0:256], 0.5, None, ALU.mult))
                    link(dve.tensor_tensor(gshift[:, :], gmean[:, :], gmean[:, :], ALU.mult))
                    dve.scalar_tensor_tensor(out=gvar[:, :], in0=ps_h[:, 256:512], scalar=0.5,
                                             in1=gshift[:, :], op0=ALU.mult, op1=ALU.subtract).then_inc(s_tab, 1)
                    dve.wait_ge(s_tab, 1)
                    link(dve.tensor_scalar(gvar[:, :], gvar[:, :], GN_EPS, None, ALU.add))
                    dve.wait_ge(s_pow, 1)
                    link(dve.tensor_tensor(gshift[:, :], gmean[:, :], grstd[:, :], ALU.mult))
                    for tab, src in ((R1, grstd), (M1, gshift)):
                        last = dve.tensor_copy(tab[:, :, :].rearrange("p k (g e) -> p (k g) e", e=CG),
                                               src[:, :].unsqueeze(2).to_broadcast([P, NT * GROUPS, CG]))
                    link(last)

                @block.tensor
                def _(pe):
                    pe.wait_ge(s_w, 16 * WEIGHT_LOADS)
                    rows = (P, CB)
                    for m in range(2):
                        for t in range(2):
                            pe.matmul(ps_g[0:rows[m], m:m + 1], raw_B[0:rows[t], t, P * m:P * m + rows[m]],
                                      l1[0:rows[t], t, 1:2], start=(t == 0), stop=(t == 1))
                    for f in range(FT):
                        for t in range(2):
                            last = pe.matmul(ps_g[:, 8 + f:9 + f], raw_1[0:rows[t], t, P * f:P * (f + 1)],
                                             l2[0:rows[t], t, 1:2], start=(t == 0), stop=(t == 1))
                    last.then_inc(s_sum, 1)
                    pe.wait_ge(s_fold, 7)
                    pe.matmul(ps_h[:, :], blockm[:, :], pm[:, :, :].rearrange("p a g -> p (a g)"),
                              start=True, stop=True).then_inc(s_sum, 1)

            xt = [sb(f"xt{b}", [P, TPC, C]) for b in range(2)]
            res = [sb(f"res{b}", [P, TPC, C]) for b in range(2)]
            xn = [sb(f"xn{b}", [P, TPC, C]) for b in range(2)]
            x1 = [sb(f"x1{b}", [P, TPC, C]) for b in range(2)]
            xn_hi = [sb(f"xn_hi{b}", [P, 2, NTOK], f32r) for b in range(2)]
            xn_lo = [sb(f"xn_lo{b}", [P, NTOK], f32r) for b in range(2)]
            h_hi = [sb(f"h_hi{b}", [P, 2, NTOK], f32r) for b in range(2)]
            h_lo = [sb(f"h_lo{b}", [P, NTOK], f32r) for b in range(2)]
            yb = sb("yb", [P, TPC, C])
            y_hi, y_lo = sb("y_hi", [P, 2, NTOK], f32r), sb("y_lo", [P, NTOK], f32r)
            gT = sb("gT", [P, FT, NTOK])
            x1sq = sb("x1sq", [P, TPC, C])
            s6a, s6b = sb("s6a", [P, TPC, 6]), sb("s6b", [P, TPC, 6])
            mva, mvb = sb("mva", [P, TPC, 2]), sb("mvb", [P, TPC, 2])
            vea, veb = sb("vea", [P, TPC]), sb("veb", [P, TPC])
            rsa, rsb = sb("rsa", [P, TPC]), sb("rsb", [P, TPC])

            ps_h = ps("ps_h", [P, 2, 512])
            ps_g = ps("ps_g", [P, 2, 512])
            ps_r = ps("ps_r", [P, 2, 512])
            ps_o = ps("ps_o", [P, 2, 512])

            def tok(t):
                return t[:, :, 0:2 * C]

            def tok_tile(t, k):
                return t[:, k // 2, (k % 2) * C:(k % 2 + 1) * C]

            def two(t):
                return t[:, :, :].rearrange("p (a b) c -> p a (b c)", b=2)

            s_init = sem("init_done")
            s_x = [sem(f"x_loaded{b}") for b in range(2)]
            s_gs, s_gn = sem("gn_scaled"), sem("gn_done")
            s_st1, s_ag1, s_ve1 = sem("ln1_stats"), sem("ln1_aggregated"), sem("ln1_var_eps")
            s_rs1, s_xn = sem("ln1_rstd"), sem("xn_ready")
            s_t1, s_xh, s_xl = sem("xn_transposed"), sem("xn_hi_ready"), sem("xn_lo_ready")
            s_scan, s_hh, s_hl = sem("scan_summed"), sem("h_hi_ready"), sem("h_lo_ready")
            s_cm, s_res, s_rsum = sem("mixed"), sem("residual_ready"), sem("residual_summed")
            s_st2, s_ag2, s_ve2 = sem("ln2_stats"), sem("ln2_aggregated"), sem("ln2_var_eps")
            s_rs2, s_y = sem("ln2_rstd"), sem("y_ready")
            s_t2, s_yh, s_yl = sem("y_transposed"), sem("y_hi_ready"), sem("y_lo_ready")
            s_w1, s_gelu = sem("hidden_summed"), sem("hidden_ready")
            s_w2, s_x1 = sem("mlp_summed"), sem("x1_ready")
            s_sq, s_acc1, s_acc2 = sem("x1_squared"), sem("x1_accumulated"), sem("x1_squares_accumulated")
            s_st = [sem(f"x1_stored{b}") for b in range(2)]
            STORES = 16 * 2 * (TPC + 3)

            def slots(engine, slot):
                for n in range(-2, 4):
                    slot(n // 2, n % 2)
                with engine.Fori(2, T - 1) as t:
                    slot(t, 0)
                    slot(t, 1)
                for n in range(STEPS - 2, STEPS + 1):
                    slot(n // 2, n % 2)

            def there(n):
                return not isinstance(n, int) or 0 <= n < STEPS

            block = ctx.enter_context(nc.Block())

            @block.sync
            def _(sp):
                def slot(t, c):
                    n = CHUNKS * t + c
                    if there(n + 2):
                        upto(sp, s_res, n + 1)
                        sp.dma_start(xt[c][:, :, :],
                                     x[TPC * c:TPC * (c + 1), :, bass.ds(t + 1, 1), :]
                                     .rearrange("k p t c -> p k (t c)")).then_inc(s_x[c], 16)
                    if there(n - 1):
                        d, u = (1 - c), (t if c else t - 1)
                        i = u // WS
                        a, b = (WS + SHIFT - 1 - i) // WS, (WS + SHIFT - 1 - u % WS) // WS
                        sp.wait_ge(s_init, 1)
                        sp.wait_ge(s_x1, n)
                        for q in range(2):
                            imgs = slice(2 * TPC * d + q, 2 * TPC * (d + 1), 2)
                            base = q * WINS
                            rows, cols = bass.ds(1 - a, CELLS), bass.ds(1 - b, CELLS)
                            row, col = bass.ds(CELLS + 1 - a, 1), bass.ds(CELLS + 1 - b, 1)
                            parts = [(x1[d][base:base + WINS, k, :],
                                      x1_cells[rows, imgs.start + 2 * k, cols, bass.ds(u, 1), :]
                                      .rearrange("r w t c -> r w (t c)")) for k in range(TPC)]
                            parts += [(x1[d][base:base + CELLS, :, :],
                                       x1_cells[row, imgs, cols, bass.ds(u, 1), :]
                                       .rearrange("r k w t c -> (r w) k (t c)")),
                                      (x1[d][base:base + WINS:CELLS, :, :],
                                       x1_cells[rows, imgs, col, bass.ds(u, 1), :]
                                       .rearrange("r k w t c -> (r w) k (t c)")),
                                      (x1[d][base:base + 1, :, :],
                                       x1_cells[row, imgs, col, bass.ds(u, 1), :]
                                       .rearrange("r k w t c -> (r w) k (t c)"))]
                            for src, dst in parts:
                                sp.dma_start(dst, src).then_inc(s_st[d], 16)

                slots(sp, slot)
                for d in range(2):
                    sp.wait_ge(s_st[d], STORES * T)

            @block.scalar
            def _(act):
                act.wait_ge(s_init, 1)

                def upper_parts(hi, full):
                    act.activation(hi[:, 0, :], full[:, 0, :], ACT.Copy)
                    return act.activation(hi[0:CB, 1, :], full[0:CB, 1, :], ACT.Copy)

                def slot(t, c):
                    n = CHUNKS * t + c
                    if there(n + 1):
                        d = 1 - c
                        act.wait_ge(s_scan, n + 2)
                        upto(act, s_cm, n)
                        for k, rows in enumerate((P, CB)):
                            last = act.activation(h_hi[d][0:rows, k, :], ps_h[0:rows, k, :], ACT.Identity,
                                                  bias=hbias[0:rows, k:k + 1])
                        last.then_inc(s_hh, 1)
                    if there(n):
                        for f in range(FT):
                            act.wait_ge(s_w1, FT * n + f + 1)
                            if f == 0:
                                upto(act, s_w2, n)
                            act.activation(gT[:, f, :], ps_g[:, f % 2, :], ACT.Gelu,
                                           bias=b1f[:, f:f + 1]).then_inc(s_gelu, 1)
                    if there(n + 2):
                        act.wait_ge(s_t1, n + 3)
                        upto(act, s_scan, n + 1)
                        upper_parts(xn_hi[c], ps_h).then_inc(s_xh, 1)
                    if there(n + 1):
                        act.wait_ge(s_t2, n + 2)
                        upper_parts(y_hi, ps_g).then_inc(s_yh, 1)

                slots(act, slot)

            @block.gpsimd
            def _(pool):
                for c in range(2):
                    pool.memset(h_hi[c][:, :, :].bitcast(fp32), 0.0)
                    last = pool.memset(h_lo[c][:, :].bitcast(fp32), 0.0)
                last.then_inc(s_init, 1)

                def slot(t, c):
                    n = CHUNKS * t + c
                    if there(n + 2):
                        pool.wait_ge(s_ve1, n + 3)
                        pool.tensor_tensor(rsa[:, :], vea[:, :], neg_half[:, 0:TPC], ALU.pow).then_inc(s_rs1, 1)
                    if there(n + 1):
                        d = 1 - c
                        pool.wait_ge(s_gs, n + 2)
                        upto(pool, s_x1, n)
                        pool.tensor_tensor(res[d][:, :, :], xt[d][:, :, :],
                                           b2b[:, :].unsqueeze(1).to_broadcast([P, TPC, C]),
                                           ALU.add).then_inc(s_res, 1)
                        pool.wait_ge(s_ve2, n + 2)
                        pool.tensor_tensor(rsb[:, :], veb[:, :], neg_half[:, 0:TPC], ALU.pow).then_inc(s_rs2, 1)
                    if there(n - 1):
                        d = 1 - c
                        pool.wait_ge(s_x1, n)
                        upto(pool, s_acc2, n - 1)
                        upto(pool, s_acc1, n - 1)
                        pool.tensor_tensor(x1sq[:, :, :], x1[d][:, :, :], x1[d][:, :, :], ALU.mult).then_inc(s_sq, 1)
                        a = acc_x[:, TPC * d:TPC * (d + 1), :]
                        pool.tensor_tensor(a, a, x1[d][:, :, :], ALU.add).then_inc(s_acc1, 1)
                        pool.wait_ge(s_sq, n)
                        a = acc_x2[:, TPC * d:TPC * (d + 1), :]
                        pool.tensor_tensor(a, a, x1sq[:, :, :], ALU.add).then_inc(s_acc2, 1)

                slots(pool, slot)

            @block.vector
            def _(dve):
                def lower_parts(hi, lo, full, bias=None):
                    for k, rows, dst in ((0, P, lo[:, :]), (1, CB, hi[CB:P, 1, :])):
                        src, up = full[0:rows, k, :], hi[0:rows, k, :]
                        if bias is None:
                            last = dve.tensor_tensor(dst, src, up, ALU.subtract)
                        else:
                            last = dve.scalar_tensor_tensor(out=dst, in0=src, scalar=bias[0:rows, k:k + 1], in1=up,
                                                            op0=ALU.add, op1=ALU.subtract)
                    return last

                def slot(t, c):
                    n = CHUNKS * t + c
                    if there(n + 1):
                        dve.wait_ge(s_hh, n + 2)
                        lower_parts(h_hi[1 - c], h_lo[1 - c], ps_h, hbias).then_inc(s_hl, 1)
                    if there(n - 1):
                        d = 1 - c
                        dve.wait_ge(s_w2, n)
                        if not isinstance(n, int) or n >= 3:
                            dve.wait_ge(s_acc2, n - 2)
                            dve.wait_ge(s_st[d], STORES * (t if c else t - 1))
                        dve.tensor_tensor(two(x1[d]), tok(ps_o), two(res[d]), ALU.add).then_inc(s_x1, 1)
                    if there(n + 2):
                        dve.wait_ge(s_x[c], 16 * (t + 2))
                        upto(dve, s_t1, n + 1)
                        r = slice(TPC * c, TPC * (c + 1))
                        dve.tensor_tensor(xn[c][:, :, :], xt[c][:, :, :], R1[:, r, :], ALU.mult).then_inc(s_gs, 1)
                        dve.wait_ge(s_gs, n + 3)
                        dve.tensor_tensor(xn[c][:, :, :], xn[c][:, :, :], M1[:, r, :],
                                          ALU.subtract).then_inc(s_gn, 1)
                        dve.wait_ge(s_gn, n + 3)
                        for k in range(TPC):
                            last = dve.bn_stats(s6a[:, k, :], xn[c][:, k, :])
                        last.then_inc(s_st1, 1)
                        dve.wait_ge(s_w, 16 * 11)
                        dve.wait_ge(s_st1, n + 3)
                        for k in range(TPC):
                            last = dve.bn_aggr(mva[:, k, :], s6a[:, k, :])
                        last.then_inc(s_ag1, 1)
                        dve.wait_ge(s_ag1, n + 3)
                        dve.tensor_scalar(vea[:, :], mva[:, :, 1], LN_EPS, None, ALU.add).then_inc(s_ve1, 1)
                        dve.wait_ge(s_rs1, n + 3)
                        for k in range(TPC):
                            last = dve.tensor_scalar(xn[c][:, k, :], xn[c][:, k, :], mva[:, k, 0:1], rsa[:, k:k + 1],
                                                     ALU.subtract, ALU.mult)
                        last.then_inc(s_xn, 1)
                    if there(n + 1):
                        d = 1 - c
                        dve.wait_ge(s_cm, n + 2)
                        for k in range(TPC):
                            last = dve.bn_stats(s6b[:, k, :], tok_tile(ps_r, k))
                        last.then_inc(s_st2, 1)
                        dve.wait_ge(s_w, 16 * 11)
                        dve.wait_ge(s_st2, n + 2)
                        for k in range(TPC):
                            last = dve.bn_aggr(mvb[:, k, :], s6b[:, k, :])
                        last.then_inc(s_ag2, 1)
                        dve.wait_ge(s_ag2, n + 2)
                        dve.tensor_scalar(veb[:, :], mvb[:, :, 1], LN_EPS, None, ALU.add).then_inc(s_ve2, 1)
                        dve.wait_ge(s_res, n + 2)
                        dve.tensor_tensor(two(res[d]), tok(ps_r), two(res[d]), ALU.add).then_inc(s_rsum, 1)
                        dve.wait_ge(s_rs2, n + 2)
                        upto(dve, s_t2, n + 1)
                        for k in range(TPC):
                            last = dve.tensor_scalar(yb[:, k, :], tok_tile(ps_r, k), mvb[:, k, 0:1], rsb[:, k:k + 1],
                                                     ALU.subtract, ALU.mult)
                        last.then_inc(s_y, 1)

                    if there(n + 2):
                        dve.wait_ge(s_xh, n + 3)
                        lower_parts(xn_hi[c], xn_lo[c], ps_h).then_inc(s_xl, 1)
                    if there(n + 1):
                        dve.wait_ge(s_yh, n + 2)
                        lower_parts(y_hi, y_lo, ps_g).then_inc(s_yl, 1)

                slots(dve, slot)

            @block.tensor
            def _(pe):
                pe.wait_ge(s_init, 1)

                def transposes(dst, src):
                    for k in range(TPC):
                        pe.transpose(dst[:, 0, P * k:P * (k + 1)], src[:, k, 0:P], ident[:, :])
                    for k in range(TPC):
                        last = pe.transpose(dst[0:CB, 1, P * k:P * (k + 1)], src[:, k, P:C], ident[:, :])
                    return last

                def slot(t, c):
                    n = CHUNKS * t + c
                    if there(n + 1):
                        d = 1 - c
                        pe.wait_ge(s_xl, n + 2)
                        upto(pe, s_hl, n)
                        for m, rows in enumerate((P, CB)):
                            cols = slice(P * m, P * m + rows)
                            terms = (*W_B.terms(xn_hi[d], xn_lo[d], cols), *W_A.terms(h_hi[d], h_lo[d], cols))
                            for k, (w, v) in enumerate(terms):
                                last = pe.matmul(ps_h[0:rows, m, :], w, v, start=(k == 0), stop=(k == len(terms) - 1))
                        last.then_inc(s_scan, 1)
                    if there(n):
                        pe.wait_ge(s_yl, n + 1)
                        for f in range(FT):
                            if f >= 2:
                                pe.wait_ge(s_gelu, FT * n + f - 1)
                            terms = W_1.terms(y_hi, y_lo, slice(P * f, P * (f + 1)))
                            for k, (w, v) in enumerate(terms):
                                last = pe.matmul(ps_g[:, f % 2, :], w, v, start=(k == 0), stop=(k == len(terms) - 1))
                            last.then_inc(s_w1, 1)
                    if there(n + 1):
                        d = 1 - c
                        pe.wait_ge(s_hl, n + 2)
                        upto(pe, s_y, n + 1)
                        upto(pe, s_rsum, n + 1)
                        for k in range(TPC):
                            terms = W_C.terms(h_hi[d], h_lo[d], slice(0, C), lambda v: v[:, P * k:P * (k + 1)])
                            for i, (w, v) in enumerate(terms):
                                last = pe.matmul(tok_tile(ps_r, k), v, w, start=(i == 0), stop=(i == len(terms) - 1))
                        last.then_inc(s_cm, 1)
                    if there(n + 2):
                        pe.wait_ge(s_xn, n + 3)
                        upto(pe, s_hl, n + 2)
                        transposes(ps_h, xn[c]).then_inc(s_t1, 1)
                    if there(n):
                        upto(pe, s_x1, n)
                        pe.wait_ge(s_gelu, FT * n + FT)
                        for k in range(TPC):
                            for f in range(FT):
                                last = pe.matmul(tok_tile(ps_o, k), gT[:, f, P * k:P * (k + 1)], w2[:, f, :],
                                                 start=(f == 0), stop=(f == FT - 1))
                        last.then_inc(s_w2, 1)
                    if there(n + 1):
                        pe.wait_ge(s_y, n + 2)
                        upto(pe, s_gelu, FT * n + FT)
                        transposes(ps_g, yb).then_inc(s_t2, 1)

                slots(pe, slot)

        bias_tab = [[top.enter_context(nc.sbuf_tensor(f"bias_{r}{k}", [P, HEADS, T], fp32)) for k in range(2)]
                    for r in range(2)]
        with ExitStack() as ctx:
            def sb(name, shape):
                return ctx.enter_context(nc.sbuf_tensor(name, shape, fp32))

            def ps(name, shape):
                return ctx.enter_context(nc.psum_tensor(name, shape, fp32))

            NG = NT * GROUPS
            RPB = (2 * WS - 1) ** 2
            hot0, hot1 = sb("hot0", [P, T, P]), sb("hot1", [RPB - P, T, P])
            tab0, tab1 = sb("tab0", [P, HEADS]), sb("tab1", [RPB - P, HEADS])
            mask = sb("mask", [P, 4, T])
            pm2 = sb("pm2", [P, 2, NG])
            mean2, var2, rstd2, shift2 = (sb(f"{w}2", [P, NG]) for w in ("mean", "var", "rstd", "shift"))
            scale_ch, shift_ch = sb("scale_ch", [P, NT, C]), sb("shift_ch", [P, NT, C])
            gcol = sb("gcol", [HALF, IMGS, 4])
            ps_m = ps("ps_m", [P, 512])
            ps_c = ps("ps_c", [P, IMGS, 2, 2])
            ps_b = ps("ps_b", [P, 2, 512])
            MB = 512 // HEADS
            s_l = sem("tables_loaded")
            s_v2, s_p2, s_m2, s_s2 = sem("gn2_steps"), sem("gn2_rstd"), sem("gn2_sums"), sem("gn2_stored")
            s_b2 = sem("bias_gathered")
            block = ctx.enter_context(nc.Block())

            @block.sync
            def _(sp):
                for dst, src in ((hot0[:, :, :], onehot[0:P]), (hot1[:, :, :], onehot[P:RPB]),
                                 (tab0[:, :], rpb[0:P]), (tab1[:, :], rpb[P:RPB]), (mask[:, :, :], shift_mask)):
                    sp.dma_start(dst, src).then_inc(s_l, 16)
                sp.wait_ge(s_v2, 9)
                for r in range(CELLS):
                    sp.dma_start(gn2_cols[r].rearrange("i p s -> p i s"), gcol[:, :, :]).then_inc(s_s2, 16)
                sp.wait_ge(s_s2, 16 * CELLS)

            @block.gpsimd
            def _(pool):
                pool.wait_ge(s_v2, 5)
                pool.tensor_tensor(rstd2[:, :], var2[:, :], neg_half[:, :], ALU.pow).then_inc(s_p2, 1)

            @block.tensor
            def _(pe):
                pe.wait_ge(s_v2, 1)
                pe.matmul(ps_m[:, :], blockm[:, :], pm2[:, :, :].rearrange("p a g -> p (a g)"),
                          start=True, stop=True).then_inc(s_m2, 1)
                pe.wait_ge(s_l, 16 * 5)
                for m in range(T):
                    dst = ps_b[:, m // MB, (m % MB) * HEADS:(m % MB + 1) * HEADS]
                    pe.matmul(dst, hot0[:, m, :], tab0[:, :], start=True, stop=False)
                    last = pe.matmul(dst, hot1[:, m, :], tab1[:, :], start=False, stop=True)
                last.then_inc(s_b2, 1)
                pe.wait_ge(s_v2, 8)
                for k in range(NT):
                    for a, tab in enumerate((scale_ch, shift_ch)):
                        for h in range(2):
                            last = pe.matmul(ps_c[0:HALF, 2 * k:2 * k + 2, a, h], tab[:, k, HALF * h:HALF * (h + 1)],
                                             ident[:, 0:WINS + 1:WINS], start=True, stop=True)
                last.then_inc(s_m2, 1)

            @block.vector
            def _(dve):
                done = [0]

                def link(ins):
                    done[0] += 1
                    ins.then_inc(s_v2, 1)
                    dve.wait_ge(s_v2, done[0])

                for k, acc in enumerate((acc_x, acc_x2)):
                    last = dve.tensor_reduce(pm2[:, k, :], acc[:, :, :].rearrange("p k (g e) -> p (k g) e", e=CG),
                                             AX.X, ALU.add)
                link(last)
                dve.wait_ge(s_m2, 1)
                per = 1.0 / (T * CG)
                link(dve.tensor_scalar(mean2[:, :], ps_m[:, 0:NG], per, None, ALU.mult))
                link(dve.tensor_tensor(shift2[:, :], mean2[:, :], mean2[:, :], ALU.mult))
                link(dve.scalar_tensor_tensor(out=var2[:, :], in0=ps_m[:, NG:2 * NG], scalar=per,
                                              in1=shift2[:, :], op0=ALU.mult, op1=ALU.subtract))
                link(dve.tensor_scalar(var2[:, :], var2[:, :], GN_EPS, None, ALU.add))
                dve.wait_ge(s_p2, 1)
                link(dve.tensor_tensor(shift2[:, :], mean2[:, :], rstd2[:, :], ALU.mult))
                link(dve.tensor_scalar(shift2[:, :], shift2[:, :], -1.0, None, ALU.mult))
                for tab, src in ((scale_ch, rstd2), (shift_ch, shift2)):
                    last = dve.tensor_copy(tab[:, :, :].rearrange("p k (g e) -> p (k g) e", e=CG),
                                           src[:, :].unsqueeze(2).to_broadcast([P, NG, CG]))
                link(last)
                dve.wait_ge(s_m2, 2)
                link(dve.tensor_copy(gcol[:, :, :], ps_c[0:HALF].rearrange("p i a h -> p i (a h)")))
                dve.wait_ge(s_b2, 1)
                for r in range(2):
                    for k in range(2):
                        for b in range(2):
                            m0, m1 = MB * b, min(MB * (b + 1), T)
                            src = ps_b[:, b, 0:(m1 - m0) * HEADS].rearrange("p (m h) -> p h m", h=HEADS)
                            msk = mask[:, 2 * r + k, m0:m1].unsqueeze(1).to_broadcast([P, HEADS, m1 - m0])
                            last = dve.tensor_tensor(bias_tab[r][k][:, :, m0:m1], src, msk, ALU.add)
                link(last)

        with ExitStack() as ctx:
            def sb(name, shape):
                return ctx.enter_context(nc.sbuf_tensor(name, shape, fp32))

            def ps(name, shape):
                return ctx.enter_context(nc.psum_tensor(name, shape, fp32))

            UW = UP * P
            NW = 2 * UP
            JP = 2 * PAIRS
            wqkv = sb("wqkv", [HALF, 2, 3 * C])
            wp = sb("wp", [HALF, 2, C])
            bqkv = sb("bqkv", [HALF, 3, 2])
            hm = sb("hm", [HALF, 5])
            bqm, bkm = sb("bqm", [HALF, 2, PAIRS]), sb("bkm", [HALF, 2, 2])
            pbb = sb("pbb", [P, C])
            xb = [sb(f"xb{b}", [P, UP, C]) for b in range(2)]
            gnc = [sb(f"gnc{b}", [HALF, 2, 2]) for b in range(2)]
            rs = [sb(f"rs{b}", [P, UP, C]) for b in range(2)]
            yo = [sb(f"yo{b}", [P, UP, C]) for b in range(2)]
            xT = sb("xT", [HALF, 2, UW])
            Qm = [sb(f"Qm{b}", [HALF, 2, PAIRS, NW, SLOT]) for b in range(2)]
            Kp = [sb(f"Kp{b}", [HALF, 2, 2, NW, T]) for b in range(2)]
            Vx = [sb(f"Vx{b}", [P, NW, JP, 2 * HD]) for b in range(2)]
            L = [sb(f"L{b}", [P, HEADS, T]) for b in range(UP)]
            E = [sb(f"E{b}", [P, HEADS, SLOT]) for b in range(UP)]
            mx = [sb(f"mx{b}", [P, HEADS]) for b in range(UP)]
            sm = [sb(f"sm{b}", [P, HEADS]) for b in range(UP)]
            ri = [sb(f"ri{b}", [P, HEADS]) for b in range(UP)]
            PT = [sb(f"PT{b}", [P, JP, P]) for b in range(2)]
            oT = [[sb(f"oT{b}{p}", [HALF, 2, 2, SLOT]) for p in range(UP)] for b in range(2)]
            ps_s = ps("ps_s", [P, 2, 512])
            ps_t = ps("ps_t", [P, 2, 512])
            ps_v = [ps(f"ps_v{b}", [P, 512]) for b in range(2)]
            ps_w = [ps(f"ps_w{b}", [P, 512]) for b in range(2)]

            s_w3, s_i3 = sem("attention_weights_loaded"), sem("attention_init")
            s_pad = sem("attention_pads_set")
            s_xb = [sem(f"unit_loaded{b}") for b in range(2)]
            s_tx, s_xT = sem("unit_transposed"), sem("unit_normed")
            s_q, s_qm = sem("q_summed"), sem("q_masked")
            s_k, s_kp = sem("k_summed"), sem("k_masked")
            s_v, s_vx = sem("v_summed"), sem("v_spread")
            s_sc, s_lg, s_mx, s_sub = sem("scores_summed"), sem("logits"), sem("row_maxima"), sem("maxima_off")
            s_ex, s_sm, s_ri, s_nm = sem("exponentials"), sem("row_sums"), sem("row_reciprocals"), sem("probabilities")
            s_pt, s_ptc = sem("probs_transposed"), sem("probs_copied")
            s_pv, s_o = sem("values_summed"), sem("heads_ready")
            s_pj, s_yo = sem("projected"), sem("unit_out_ready")
            s_rs = sem("unit_residual")
            s_so = [sem(f"unit_stored{b}") for b in range(2)]
            LOADS = 2 + 1
            block = ctx.enter_context(nc.Block())

            def units(engine, slot):
                last_row = IMGS * (CELLS - 1)
                for u in range(-1, 4):
                    slot(u // 2, u % 2, 0)
                with engine.Fori(2, last_row // 2) as i:
                    slot(i, 0, 0)
                    slot(i, 1, 0)
                with engine.Fori(last_row // 2, UNITS // 2 - 1) as i:
                    slot(i, 0, 1)
                    slot(i, 1, 1)
                for u in (UNITS - 2, UNITS - 1, UNITS):
                    slot(u // 2, u % 2, 1)

            def is_unit(u):
                return not isinstance(u, int) or 0 <= u < UNITS

            def lagged(u, c, p):
                return (u, c, p - 2) if p >= 2 else (u - 1, 1 - c, p + 2)

            @block.sync
            def _(sp):
                for dst, src in ((wqkv[:, :, :], qkvT.rearrange("(h p) n -> p h n", h=2)),
                                 (wp[:, :, :], projT.rearrange("(h p) n -> p h n", h=2)),
                                 (bqkv[:, :, :], qkv_b),
                                 (hm[:, :], head_masks), (pbb[:, :], proj_b.partition_broadcast(P))):
                    sp.dma_start(dst, src).then_inc(s_w3, 16)
                sp.wait_ge(s_pad, 1)

                x1_rows = x1_cells.rearrange("r k w t c -> (r k) w t c")
                cols = gn2_cols.rearrange("r k p s -> (r k) p s")

                def load(i, c):
                    u = 2 * i + c
                    for w in range(2):
                        src = x1_rows[bass.ds(u + IMGS, 1), w + 1:w + 2 * UP:2, :, :].rearrange("u w t c -> (u t) w c")
                        sp.dma_start(xb[c][SLOT * w:SLOT * w + T, :, :], src).then_inc(s_xb[c], 16)
                    sp.dma_start(gnc[c][:, :, :].rearrange("p s h -> p (s h)"),
                                 cols[bass.ds(u, 1), :, :].rearrange("u p s -> (u p) s"))\
                      .then_inc(s_xb[c], 16)

                def slot(i, c, r):
                    u = 2 * i + c
                    if is_unit(u + 2):
                        upto(sp, s_rs, u + 1)
                        upto(sp, s_xT, 2 * u + 2)
                        load(i + 1, c)
                    if is_unit(u - 1):
                        d = 1 - c
                        sp.wait_ge(s_yo, 2 * u)
                        for w in range(2):
                            src = yo[d][SLOT * w:SLOT * w + T, :, :]
                            sp.dma_start(out[bass.ds(u - 1, 1), :, w, :, :].rearrange("u p t c -> (u t) p c"), src)\
                              .then_inc(s_so[d], 16)

                load(0, 0)
                units(sp, slot)
                for d in range(2):
                    sp.wait_ge(s_so[d], 32 * UNITS // 2)

            @block.gpsimd
            def _(pool):
                for b in range(2):
                    pool.memset(xb[b][:, :, :], 0.0)
                    pool.memset(Qm[b][:, :, :, :, :], 0.0)
                    for p in range(UP):
                        pool.memset(oT[b][p][:, :, :, :], 0.0)
                pool.memset(rs[0][:, :, :], 0.0).then_inc(s_pad, 1)
                pool.wait_ge(s_w3, 16 * 5)

                def norm(u, p):
                    k = UP * u + p
                    pool.wait_ge(s_ri, k + 1)
                    e = E[p][:, :, 0:T]
                    pool.tensor_tensor(e, e, ri[p][:, :].unsqueeze(2).to_broadcast([P, HEADS, T]), ALU.mult)\
                        .then_inc(s_nm, 1)

                def slot(i, c, r):
                    u = 2 * i + c
                    for p in range(UP):
                        pu, pp = (u, p - 1) if p else (u - 1, UP - 1)
                        if is_unit(pu):
                            norm(pu, pp)
                        if is_unit(u) and p == 0:
                            pool.wait_ge(s_xb[c], 16 * LOADS * (i + 1))
                            upto(pool, s_yo, 2 * (u - 1))
                            pool.tensor_tensor(rs[c][:, :, :], xb[c][:, :, :],
                                               pbb[:, :].unsqueeze(1).to_broadcast([P, UP, C]), ALU.add)\
                                .then_inc(s_rs, 1)

                units(pool, slot)

            @block.scalar
            def _(act):
                act.wait_ge(s_w3, 16 * 5)
                act.wait_ge(s_i3, 2)
                act.wait_ge(s_pad, 1)

                def normed(i, c, h):
                    v, d = 2 * i + c + 1, 1 - c
                    act.wait_ge(s_tx, 2 * v + h + 1)
                    if h == 0:
                        upto(act, s_v, 2 * v)
                    act.activation(xT[:, h, :], ps_w[h][0:HALF, :], ACT.Identity,
                                   scale=gnc[d][:, 0, h:h + 1], bias=gnc[d][:, 1, h:h + 1]).then_inc(s_xT, 1)

                def query(i, c, h):
                    v, d = 2 * i + c + 1, 1 - c
                    act.wait_ge(s_q, 2 * v + h + 1)
                    if h == 0:
                        upto(act, s_sc, UP * (v - 1))
                    for j in range(PAIRS):
                        last = act.activation(Qm[d][:, h, j, :, 0:T],
                                              ps_w[1 - h][0:HALF, 0:NW * T].rearrange("p (w t) -> p w t", t=T),
                                              ACT.Identity, scale=hm[:, j:j + 1], bias=bqm[:, h, j:j + 1])
                    last.then_inc(s_qm, 1)

                def key(i, c, h):
                    v, d = 2 * i + c + 1, 1 - c
                    act.wait_ge(s_k, 2 * v + h + 1)
                    for e in range(2):
                        last = act.activation(Kp[d][:, h, e, :, :],
                                              ps_w[1 - h][0:HALF, 0:NW * T].rearrange("p (w t) -> p w t", t=T),
                                              ACT.Identity, scale=hm[:, PAIRS + e:PAIRS + e + 1],
                                              bias=bkm[:, h, e:e + 1])
                    last.then_inc(s_kp, 1)

                def slot(i, c, r):
                    u = 2 * i + c
                    nxt = is_unit(u + 1)
                    for p in range(UP):
                        lu, lc, lp = lagged(u, c, p)
                        k = UP * u + p - 2
                        if is_unit(lu):
                            act.wait_ge(s_pt, k + 1)
                            upto(act, s_pv, k - 1)
                            act.activation(PT[lp % 2][:, :, :].rearrange("p (a b) q -> p a (b q)", a=2),
                                           ps_t[:, :, 0:PAIRS * P], ACT.Copy).then_inc(s_ptc, 1)
                        if nxt and p == 0:
                            normed(i, c, 0)
                            normed(i, c, 1)
                        if nxt and p == 1:
                            query(i, c, 0)
                            query(i, c, 1)
                        if nxt and p == 2:
                            key(i, c, 1)
                        if is_unit(lu):
                            act.wait_ge(s_pv, k + 1)
                            upto(act, s_pj, 2 * (lu - 1))
                            for h in range(2):
                                src = ps_v[lp % 2][0:HALF, h * P:(h + 1) * P].rearrange("p (w t) -> p w t", w=2)
                                last = act.activation(oT[lc][lp][:, h, :, 0:T], src[:, :, 0:T], ACT.Identity,
                                                      bias=bqkv[:, 2, h:h + 1])
                            last.then_inc(s_o, 1)
                        if is_unit(u):
                            k = UP * u + p
                            act.wait_ge(s_sub, k + 1)
                            upto(act, s_pt, k - 3)
                            act.activation(E[p][:, :, 0:T], L[p][:, :, :], ACT.Exp).then_inc(s_ex, 1)
                        if nxt and p == 1:
                            key(i, c, 0)

                units(act, slot)

            @block.vector
            def _(dve):
                for b in range(2):
                    dve.memset(Vx[b][:, :, :, :], 0.0)
                for p in range(UP):
                    last = dve.memset(E[p][:, :, :], 0.0)
                last.then_inc(s_i3, 1)
                dve.wait_ge(s_w3, 16 * 5)
                for h in range(2):
                    dve.tensor_scalar(bqm[:, h, :], hm[:, 0:PAIRS], bqkv[:, 0, h:h + 1], None, ALU.mult)
                    last = dve.tensor_scalar(bkm[:, h, :], hm[:, PAIRS:PAIRS + 2], bqkv[:, 1, h:h + 1], None, ALU.mult)
                last.then_inc(s_i3, 1)
                dve.wait_ge(s_i3, 2)

                def spread(i, c, half):
                    v, d = 2 * i + c + 1, 1 - c
                    dve.wait_ge(s_v, 2 * v + half + 1)
                    if half == 0:
                        upto(dve, s_pv, UP * (v - 1))
                    for w in range(2):
                        for e in range(2):
                            src = ps_w[1 - half][SLOT * w:SLOT * (w + 1), 0:2 * C]\
                                .rearrange("p (a j e) -> p a j e", a=2, j=JP)[:, :, :, HD * e:HD * (e + 1)]
                            last = dve.tensor_copy(
                                Vx[d][SLOT * e:SLOT * (e + 1), 4 * half + w:4 * half + w + 3:2, :, HD * e:HD * (e + 1)],
                                src)
                    last.then_inc(s_vx, 1)

                def finish(i, c, half):
                    v, d = 2 * i + c - 1, 1 - c
                    dve.wait_ge(s_pj, 2 * v + half + 1)
                    if half == 0:
                        dve.wait_ge(s_rs, v + 1)
                        upto(dve, s_so[d], 32 * (i if c else i - 1))
                    ab = slice(2 * half, 2 * half + 2)
                    dve.tensor_tensor(yo[d][:, ab, :], ps_w[half][:, 0:2 * C].rearrange("p (a c) -> p a c", a=2),
                                      rs[d][:, ab, :], ALU.add).then_inc(s_yo, 1)

                def slot(i, c, r):
                    u = 2 * i + c
                    nxt = is_unit(u + 1)
                    for p in range(UP):
                        pu, pp = (u, p - 1) if p else (u - 1, UP - 1)
                        if is_unit(pu):
                            k = UP * u + p - 1
                            dve.wait_ge(s_ex, k + 1)
                            dve.tensor_reduce(sm[pp][:, :], E[pp][:, :, 0:T], AX.X, ALU.add).then_inc(s_sm, 1)
                            dve.wait_ge(s_sm, k + 1)
                            dve.reciprocal(ri[pp][:, :], sm[pp][:, :]).then_inc(s_ri, 1)
                        if nxt and p == 3:
                            spread(i, c, 1)
                        if is_unit(u):
                            k = UP * u + p
                            dve.wait_ge(s_sc, k + 1)
                            tab = bias_tab[r][p // (UP - 1)][:, :, :].rearrange("p (a h) m -> p a (h m)", a=2)
                            dve.scalar_tensor_tensor(out=L[p][:, :, :].rearrange("p (a h) m -> p a (h m)", a=2),
                                                     in0=ps_s[:, :, 0:HEADS // 2 * T], scalar=HD ** -0.5,
                                                     in1=tab, op0=ALU.mult, op1=ALU.add).then_inc(s_lg, 1)
                            dve.wait_ge(s_lg, k + 1)
                            dve.tensor_reduce(mx[p][:, :], L[p][:, :, :], AX.X, ALU.max).then_inc(s_mx, 1)
                            dve.wait_ge(s_mx, k + 1)
                            dve.tensor_tensor(L[p][:, :, :], L[p][:, :, :],
                                              mx[p][:, :].unsqueeze(2).to_broadcast([P, HEADS, T]),
                                              ALU.subtract).then_inc(s_sub, 1)
                        if nxt and p == 2:
                            spread(i, c, 0)
                        if is_unit(u - 1) and p in (0, 3):
                            finish(i, c, p // 3)

                units(dve, slot)

            @block.tensor
            def _(pe):
                pe.wait_ge(s_w3, 16 * 5)
                pe.wait_ge(s_i3, 2)
                pe.wait_ge(s_pad, 1)

                def turn(i, c, h):
                    v, d = 2 * i + c + 1, 1 - c
                    if h == 0:
                        pe.wait_ge(s_xb[d], 16 * LOADS * (i + 1 if c == 0 else i + 2))
                        upto(pe, s_vx, 2 * v)
                    else:
                        upto(pe, s_yo, 2 * (v - 2))
                    for p in range(UP):
                        last = pe.transpose(ps_w[h][0:HALF, P * p:P * (p + 1)],
                                            xb[d][:, p, HALF * h:HALF * (h + 1)], ident[:, :])
                    last.then_inc(s_tx, 1)

                def project(h, part, done):
                    for k in range(2):
                        last = pe.matmul(ps_w[1 - h][0:HALF, 0:NW * T].rearrange("p (w t) -> p w t", t=T),
                                         wqkv[:, k, C * part + HALF * h:C * part + HALF * (h + 1)],
                                         xT[:, k, :].rearrange("p (w t) -> p w t", t=SLOT)[:, :, 0:T],
                                         start=(k == 0), stop=(k == 1))
                    last.then_inc(done, 1)

                def query(v, h):
                    if h == 0:
                        pe.wait_ge(s_xT, 2 * v + 2)
                    else:
                        upto(pe, s_yo, 2 * (v - 2) + 1)
                    project(h, 0, s_q)

                def key(v, h):
                    pe.wait_ge(s_qm, 2 * v + h + 1)
                    project(h, 1, s_k)

                def values(v, half):
                    pe.wait_ge(s_kp, 2 * v + half + 1)
                    for a in range(2):
                        p = 2 * half + a
                        for k in range(2):
                            last = pe.matmul(ps_w[1 - half][:, C * a:C * (a + 1)], xT[:, k, P * p:P * (p + 1)],
                                             wqkv[:, k, 2 * C:3 * C], start=(k == 0), stop=(k == 1))
                    last.then_inc(s_v, 1)

                def mix(i, c, half):
                    v, d = 2 * i + c - 1, 1 - c
                    pe.wait_ge(s_o, UP * v + 2 * half + 2)
                    if is_unit(v + 2):
                        if half == 0:
                            pe.wait_ge(s_xT, 2 * (v + 2) + 1)
                        else:
                            pe.wait_ge(s_vx, 2 * (v + 2) + 1)
                    else:
                        pe.wait_ge(s_vx, 2 * UNITS)
                        pe.wait_ge(s_yo, 2 * (v - 1) + half + 1)
                    for a in range(2):
                        p = 2 * half + a
                        for k in range(2):
                            last = pe.matmul(ps_w[half][:, C * a:C * (a + 1)],
                                             oT[d][p][:, k, :, :].rearrange("p w t -> p (w t)"),
                                             wp[:, k, :], start=(k == 0), stop=(k == 1))
                    last.then_inc(s_pj, 1)

                def slot(i, c, r):
                    u = 2 * i + c
                    v = u + 1
                    nxt = is_unit(v)
                    for p in range(UP):
                        lu, lc, lp = lagged(u, c, p)
                        if is_unit(lu):
                            k = UP * u + p - 2
                            pe.wait_ge(s_nm, k + 1)
                            upto(pe, s_ptc, k)
                            for j in range(JP):
                                last = pe.transpose(ps_t[:, j // PAIRS, P * (j % PAIRS):P * (j % PAIRS + 1)],
                                                    E[lp][:, 2 * j:2 * j + 2, :].rearrange("p h m -> p (h m)"),
                                                    ident[:, :])
                            last.then_inc(s_pt, 1)
                        if nxt:
                            if p == 0:
                                turn(i, c, 0)
                            if p == 1:
                                query(v, 0)
                            if p == 2:
                                key(v, 1)
                            if p == 3:
                                values(v, 1)
                        if is_unit(u):
                            k = UP * u + p
                            if p == 0:
                                pe.wait_ge(s_qm, 2 * u + 2)
                                pe.wait_ge(s_kp, 2 * u + 2)
                            upto(pe, s_lg, k)
                            for w in range(2):
                                for h in range(2):
                                    for j in range(PAIRS):
                                        last = pe.matmul(ps_s[SLOT * w:SLOT * (w + 1), h, 2 * T * j:2 * T * (j + 1)],
                                                         Qm[c][:, h, j, 2 * p + w, :],
                                                         Kp[c][:, h, :, 2 * p + w, :], start=True, stop=True)
                            last.then_inc(s_sc, 1)
                        if nxt and p == 0:
                            turn(i, c, 1)
                        if nxt and p == 1:
                            query(v, 1)
                        if nxt and p == 2:
                            values(v, 0)
                        if is_unit(lu):
                            k = UP * u + p - 2
                            pe.wait_ge(s_ptc, k + 1)
                            pe.wait_ge(s_vx, 2 * lu + 2)
                            upto(pe, s_o, k - 1)
                            for w in range(2):
                                for h in range(2):
                                    for j in range(PAIRS):
                                        last = pe.matmul(
                                            ps_v[lp % 2][2 * HD * j:2 * HD * (j + 1),
                                                         P * h + SLOT * w:P * h + SLOT * w + T],
                                            Vx[lc][:, 2 * lp + w, PAIRS * h + j, :],
                                            PT[lp % 2][:, PAIRS * h + j, SLOT * w:SLOT * w + T],
                                            start=True, stop=True)
                            last.then_inc(s_pv, 1)
                        if nxt and p == 1:
                            key(v, 0)
                        if is_unit(u - 1) and p in (0, 3):
                            mix(i, c, p // 3)

                units(pe, slot)



def by_window(a):
    a = np.asarray(a).reshape(NT, 2, CELLS, WS, CELLS, WS, C)
    return np.ascontiguousarray(a.transpose(0, 1, 2, 4, 3, 5, 6).reshape(NT, P, T, C))


def by_column(*vectors, rows):
    return np.ascontiguousarray(np.stack([np.asarray(v).reshape(-1, rows).T for v in vectors], 2))


def from_units(a):
    tok = np.array(cell_tokens())
    row = (WS * (np.arange(CELLS)[:, None] + tok[:, 0]) + tok[:, 2]) % SIDE
    col = (WS * (np.arange(CELLS)[:, None] + tok[:, 1]) + tok[:, 3]) % SIDE
    a = np.asarray(a).reshape(CELLS, IMGS, CELLS, T, C)
    y = np.empty((IMGS, SIDE, SIDE, C), a.dtype)
    y[np.arange(IMGS)[None, :, None, None], row[:, None, None, :], col[None, None, :, :]] = a
    return y


def shape_constants():
    f = np.float32
    part = np.arange(P)
    block_mean = ((part[:, None] // WINS) == (part[None, :] // WINS)).astype(f) / WINS
    ch = np.arange(HALF)
    masks = np.stack([(ch // (2 * HD) == j) for j in range(PAIRS)] + [(ch // HD % 2 == e) for e in range(2)], 1)
    tok = np.array(cell_tokens())
    yi = WS * tok[:, 0] + tok[:, 2] - SHIFT
    xi = WS * tok[:, 1] + tok[:, 3] - SHIFT
    rel = (yi[:, None] - yi[None, :] + WS - 1) * (2 * WS - 1) + xi[:, None] - xi[None, :] + WS - 1
    onehot = np.zeros(((2 * WS - 1) ** 2, T, P), f)
    for w in range(2):
        onehot[rel.T, np.arange(T)[:, None], SLOT * w + np.arange(T)[None, :]] = 1
    mask = np.zeros((P, 2, 2, T), f)
    for r in range(2):
        for k in range(2):
            for w in range(2):
                apart = np.zeros((T, T), bool)
                if r:
                    apart |= tok[:, None, 0] != tok[None, :, 0]
                if k and w:
                    apart |= tok[:, None, 1] != tok[None, :, 1]
                mask[SLOT * w:SLOT * w + T, r, k] = np.where(apart, -100.0, 0.0)
    return {"block_mean": block_mean, "identity": np.eye(P, dtype=f), "head_masks": masks.astype(f),
            "onehot": onehot, "shift_mask": mask.reshape(P, 4, T)}


def kernel(**inputs):
    import concourse.bacc as bacc
    from concourse.bass_utils import run_bass_kernel_spmd

    def plain(name):
        return np.ascontiguousarray(inputs[name])

    arrays = {"x": by_window(inputs["x"])}
    twice = np.r_[0:C, P:C]
    for name in ("W2", "b2"):
        arrays[name] = plain("L0_conv_" + name)
    for name in ("A", "Bm", "Cm", "W1"):
        arrays[name] = np.ascontiguousarray(np.asarray(inputs["L0_conv_" + name])[twice])
    for name in ("ln1", "ln2"):
        arrays[name] = by_column(*(np.asarray(inputs[f"L0_conv_{name}_{k}"])[twice] for k in "wb"), rows=P)
    arrays["b1"] = by_column(inputs["L0_conv_b1"], rows=P)[:, :, 0]
    arrays["qkvT"] = np.ascontiguousarray(np.asarray(inputs["L1_conv_qkv_w"]).T)
    arrays["qkv_b"] = by_column(inputs["L1_conv_qkv_b"], rows=HALF)[:, :, 0].reshape(HALF, 3, 2)
    arrays["projT"] = np.ascontiguousarray(np.asarray(inputs["L1_conv_proj_w"]).T)
    arrays["proj_b"] = plain("L1_conv_proj_b")
    arrays["rpb"] = plain("L1_conv_rpb_table")
    arrays.update(shape_constants())
    nc = bacc.Bacc("TRN2", target_bir_lowering=False, num_devices=1)
    args = {n: nc.dram_tensor("in_" + n, a.shape, fp32, kind="ExternalInput").ap() for n, a in arrays.items()}
    out = nc.dram_tensor("out", (UNITS, UP, 2, T, C), fp32, kind="ExternalOutput").ap()
    build(nc, **args, out=out)
    r = run_bass_kernel_spmd(nc, [{"in_" + n: a for n, a in arrays.items()}], core_ids=[0])
    return from_units(r.results[0]["out"])
```

```python
from contextlib import ExitStack

import numpy as np

import concourse.bass as bass
from concourse import mybir

fp32 = mybir.dt.float32
f32r = mybir.dt.float32r
ALU = mybir.AluOpType
ACT = mybir.ActivationFunctionType
AX = mybir.AxisListType

IMGS, SIDE, C = 16, 56, 192
WS = 7
CELLS = SIDE // WS
WINS = CELLS * CELLS
T = WS * WS
SHIFT = 3
GROUPS, CG = 32, C // 32
HID = 4 * C
HEADS, HD = 12, 16
P = 128
CB = C - P
JP = HEADS // 2
NT = IMGS // 2
TPC = 4
CHUNKS = NT // TPC
NTOK = TPC * P
FT = HID // P
STEPS = T * CHUNKS
GN_EPS = LN_EPS = 1e-5
UNITS = CELLS * IMGS
SLOT = 64
UP = CELLS // 2
CROW = CELLS + 2


def cell_tokens():
    return [(int(i < SHIFT), int(j < SHIFT), i, j) for i in range(WS) for j in range(WS)]


def upto(engine, semaphore, count):
    if isinstance(count, int) and count <= 0:
        return
    engine.wait_ge(semaphore, count)


def build(nc, x, A, Bm, Cm, ln1, ln2, W1, b1, W2, b2,
          qkvT, qkv_b, projT, proj_b, rpb, image_mean, identity, head_masks, onehot, shift_mask, out):
    top = ExitStack()

    def sem(name):
        return top.enter_context(nc.semaphore(name))

    with top:
        x1_cells = nc.dram_tensor("x1_cells", [CROW, IMGS, CROW, T, C], fp32).ap()
        gn2_rows = nc.dram_tensor("gn2_rows", [IMGS, 2, C], fp32).ap()
        TH = P // GROUPS

        def keep(name, shape):
            return top.enter_context(nc.sbuf_tensor(name, shape, fp32))

        ident = keep("ident", [P, P])
        img_mean = keep("img_mean", [P, 2])
        neg_half = keep("neg_half", [P, TPC])
        acc_x = keep("acc_x", [P, NT, C])
        acc_x2 = keep("acc_x2", [P, NT, C])

        class Split:

            def __init__(self, ctx, name, cols):
                self.parts = [ctx.enter_context(nc.sbuf_tensor(f"{name}_{k}", [P, cols], f32r))
                              for k in ("a_hi", "a_lo", "b_hi", "b_lo")]

            def terms(self, data_hi, data_lo, cols, pick=lambda t: t):
                a_hi, a_lo, b_hi, b_lo = (w[:, cols] for w in self.parts)
                da, db, dl = pick(data_hi[:, 0, :]), pick(data_hi[:, 1, :]), pick(data_lo[:, :])
                return (a_hi, da), (a_hi, dl), (a_lo, da), (b_hi, db), (b_lo, db)

        with ExitStack() as ctx:
            def sb(name, shape, dt=fp32, where=ctx):
                return where.enter_context(nc.sbuf_tensor(name, shape, dt))

            def ps(name, shape, where=ctx):
                return where.enter_context(nc.psum_tensor(name, shape, fp32))

            R1 = sb("R1", [P, NT, C])
            M1 = sb("M1", [P, NT, C])
            W_B, W_A, W_C = (Split(ctx, name, C) for name in ("wB", "wA", "wC"))
            W_1 = Split(ctx, "w1", HID)
            w2 = sb("w2", [P, FT, 2, C], f32r)
            b2b = sb("b2b", [P, C])
            b1f = sb("b1f", [P, FT])
            hbias = sb("hbias", [P, 2])
            s_w = sem("weights_loaded")
            WEIGHT_LOADS = 11

            with ExitStack() as pre:
                XS = 3
                xs = [sb(f"xs{b}", [P, T, C], where=pre) for b in range(XS)]
                st = sb("st", [P, NT * GROUPS, 6], where=pre)
                pm = sb("pm", [P, 2, NT * GROUPS], where=pre)
                sq = sb("sq", [P, 2, NT * GROUPS], where=pre)
                gmean, gvar = (sb(f"g{w}", [P, 2, 2], where=pre) for w in ("mean", "var"))
                gtab = sb("gtab", [P, 2, 2, 2], where=pre)
                gwide = sb("gwide", [P, 8, WINS], where=pre)
                raw_B, raw_A, raw_C, fold_B = (sb(name, [P, 2, C], where=pre)
                                               for name in ("raw_B", "raw_A", "raw_C", "fold_B"))
                raw_2 = sb("raw_2", [P, FT, C], where=pre)
                raw_1, fold_1 = sb("raw_1", [P, 2, HID], where=pre), sb("fold_1", [P, 2, HID], where=pre)
                l1, l2 = sb("l1", [P, 2, 2], where=pre), sb("l2", [P, 2, 2], where=pre)
                b1c = sb("b1c", [P, FT], where=pre)
                ps_g, ps_h = ps("ps_g0", [P, 512], where=pre), ps("ps_h0", [P, 512], where=pre)
                s_xs = [sem(f"stat_rows_loaded{b}") for b in range(XS)]
                s_bn = sem("stat_rows_used")
                s_fold = sem("folded")
                s_sum = sem("group_sums")
                s_pow = sem("group_rstd")
                s_tab = sem("group_tables")
                s_i0 = sem("exponents_set")
                s_wh = sem("weight_upper_parts")
                block = pre.enter_context(nc.Block())

                @block.sync
                def _(sp):
                    for k in range(NT):
                        if k >= XS:
                            sp.wait_ge(s_bn, k - XS + 1)
                        sp.dma_start(xs[k % XS][:, :, :], x[k]).then_inc(s_xs[k % XS], 16)

                @block.scalar
                def _(act):
                    for dst, src in ((ident[:, :], identity), (img_mean[:, :], image_mean),
                                     (raw_2[:, :, :], W2.rearrange("(f p) n -> p f n", p=P)),
                                     (b2b[:, :], b2.partition_broadcast(P)),
                                     (l1[:, :, :], ln1), (l2[:, :, :], ln2), (b1c[:, :], b1)):
                        act.dma_start(dst, src).then_inc(s_w, 16)
                    for raw, src in ((raw_B, Bm), (raw_A, A), (raw_C, Cm), (raw_1, W1)):
                        act.dma_start(raw[:, :, :], src.rearrange("(k p) n -> p k n", p=P)).then_inc(s_w, 16)
                    act.wait_ge(s_fold, 1)
                    for full, parts in ((fold_B, W_B), (raw_A, W_A), (raw_C, W_C), (fold_1, W_1)):
                        for t in range(2):
                            act.activation(parts.parts[2 * t][:, :], full[:, t, :], ACT.Copy)
                    act.activation(w2[:, :, 0, :], raw_2[:, :, :], ACT.Copy).then_inc(s_wh, 1)

                @block.gpsimd
                def _(pool):
                    pool.memset(acc_x[:, :, :], 0.0)
                    pool.memset(acc_x2[:, :, :], 0.0)
                    pool.memset(neg_half[:, :], -0.5).then_inc(s_i0, 1)
                    pool.wait_ge(s_i0, 1)
                    pool.wait_ge(s_wh, 1)
                    for full, parts in ((fold_B, W_B), (raw_A, W_A), (raw_C, W_C), (fold_1, W_1)):
                        for t in range(2):
                            pool.tensor_tensor(parts.parts[2 * t + 1][:, :], full[:, t, :],
                                               parts.parts[2 * t][:, :], ALU.subtract)
                    pool.tensor_tensor(w2[:, :, 1, :], raw_2[:, :, :], w2[:, :, 0, :], ALU.subtract)
                    pool.wait_ge(s_fold, 11)
                    pool.tensor_tensor(gtab[:, 0, :, :], gvar[:, :, :],
                                       neg_half[:, :].rearrange("p (a b) -> p a b", a=2), ALU.pow).then_inc(s_pow, 1)

                @block.vector
                def _(dve):
                    fold = [0]

                    def link(ins):
                        fold[0] += 1
                        ins.then_inc(s_fold, 1)
                        dve.wait_ge(s_fold, fold[0])

                    for k in range(NT):
                        if k == NT // 2:
                            dve.wait_ge(s_w, 16 * WEIGHT_LOADS)
                            for t in range(2):
                                dve.tensor_scalar(fold_B[:, t, :], raw_B[:, t, :], l1[:, t, 0:1], None, ALU.mult)
                                last = dve.tensor_scalar(fold_1[:, t, :], raw_1[:, t, :], l2[:, t, 0:1], None,
                                                         ALU.mult)
                            link(last)
                        dve.wait_ge(s_xs[k % XS], 16 * (k // XS + 1))
                        for g in range(GROUPS):
                            last = dve.bn_stats(st[:, GROUPS * k + g, :], xs[k % XS][:, :, CG * g:CG * (g + 1)])
                        last.then_inc(s_bn, 1)
                    dve.wait_ge(s_bn, NT)
                    per = T * CG / 2
                    link(dve.tensor_tensor(pm[:, 0, :], st[:, :, 1], st[:, :, 4], ALU.add))
                    link(dve.tensor_tensor(sq[:, 0, :], st[:, :, 1], st[:, :, 1], ALU.mult))
                    link(dve.tensor_tensor(sq[:, 1, :], st[:, :, 4], st[:, :, 4], ALU.mult))
                    link(dve.tensor_tensor(sq[:, 0, :], sq[:, 0, :], sq[:, 1, :], ALU.add))
                    link(dve.tensor_tensor(sq[:, 1, :], st[:, :, 2], st[:, :, 5], ALU.add))
                    link(dve.scalar_tensor_tensor(out=pm[:, 1, :], in0=sq[:, 1, :], scalar=1.0 / per,
                                                  in1=sq[:, 0, :], op0=ALU.mult, op1=ALU.add))
                    dve.wait_ge(s_sum, 1)
                    dve.tensor_copy(hbias[:, 0:1], ps_g[:, 0:1])
                    dve.tensor_copy(hbias[0:CB, 1:2], ps_g[0:CB, 1:2])
                    link(dve.tensor_tensor(b1f[:, :], ps_g[:, 8:8 + FT], b1c[:, :], ALU.add))
                    dve.wait_ge(s_sum, 2)
                    sums = ps_h[:, 0:8].rearrange("p (a h q) -> p a h q", a=2, h=2)
                    link(dve.tensor_scalar(gmean[:, :, :], sums[:, 0], 0.5, None, ALU.mult))
                    link(dve.tensor_tensor(gtab[:, 1, :, :], gmean[:, :, :], gmean[:, :, :], ALU.mult))
                    dve.scalar_tensor_tensor(out=gvar[:, :, :], in0=sums[:, 1], scalar=0.5,
                                             in1=gtab[:, 1, :, :], op0=ALU.mult, op1=ALU.subtract).then_inc(s_tab, 1)
                    dve.wait_ge(s_tab, 1)
                    link(dve.tensor_scalar(gvar[:, :, :], gvar[:, :, :], GN_EPS, None, ALU.add))
                    dve.wait_ge(s_pow, 1)
                    link(dve.tensor_tensor(gtab[:, 1, :, :], gmean[:, :, :], gtab[:, 0, :, :], ALU.mult))
                    link(dve.tensor_copy(gwide[:, :, :], gtab[:, :, :, :].rearrange("p a h q -> p (a h q)")
                                         .unsqueeze(2).to_broadcast([P, 8, WINS])))
                    dve.wait_ge(s_sum, 3)
                    for a, tab in enumerate((R1, M1)):
                        last = dve.tensor_copy(tab[:, :, :].rearrange("p k (g e) -> p (k g) e", e=CG),
                                               ps_g[:, 256 * a:256 * (a + 1)].unsqueeze(2)
                                               .to_broadcast([P, NT * GROUPS, CG]))
                    link(last)

                @block.tensor
                def _(pe):
                    pe.wait_ge(s_w, 16 * WEIGHT_LOADS)
                    rows = (P, CB)
                    for m in range(2):
                        for t in range(2):
                            pe.matmul(ps_g[0:rows[m], m:m + 1], raw_B[0:rows[t], t, P * m:P * m + rows[m]],
                                      l1[0:rows[t], t, 1:2], start=(t == 0), stop=(t == 1))
                    for f in range(FT):
                        for t in range(2):
                            last = pe.matmul(ps_g[:, 8 + f:9 + f], raw_1[0:rows[t], t, P * f:P * (f + 1)],
                                             l2[0:rows[t], t, 1:2], start=(t == 0), stop=(t == 1))
                    last.then_inc(s_sum, 1)
                    pe.wait_ge(s_fold, 7)
                    for a in range(2):
                        for h in range(2):
                            last = pe.matmul(ps_h[:, 4 * a + 2 * h:4 * a + 2 * h + 2],
                                             pm[:, a, P * h:P * (h + 1)], img_mean[:, :], start=True, stop=True)
                    last.then_inc(s_sum, 1)
                    pe.wait_ge(s_fold, 13)
                    for a in range(2):
                        for h in range(2):
                            last = pe.matmul(ps_g[:, 256 * a + P * h:256 * a + P * (h + 1)],
                                             gwide[:, 4 * a + 2 * h:4 * a + 2 * h + 2, :].rearrange("p q w -> p (q w)"),
                                             ident[:, :], start=True, stop=True)
                    last.then_inc(s_sum, 1)

            xt = [sb(f"xt{b}", [P, TPC, C]) for b in range(2)]
            res = [sb(f"res{b}", [P, TPC, C]) for b in range(2)]
            xn = [sb(f"xn{b}", [P, TPC, C]) for b in range(2)]
            x1 = [sb(f"x1{b}", [P, TPC, C]) for b in range(2)]
            xn_hi = [sb(f"xn_hi{b}", [P, 2, NTOK], f32r) for b in range(2)]
            xn_lo = [sb(f"xn_lo{b}", [P, NTOK], f32r) for b in range(2)]
            h_hi = [sb(f"h_hi{b}", [P, 2, NTOK], f32r) for b in range(2)]
            h_lo = [sb(f"h_lo{b}", [P, NTOK], f32r) for b in range(2)]
            yb = sb("yb", [P, TPC, C])
            y_hi, y_lo = sb("y_hi", [P, 2, NTOK], f32r), sb("y_lo", [P, NTOK], f32r)
            gF = [sb(f"gF{b}", [P, NTOK]) for b in range(4)]
            g_hi, g_lo = (sb(name, [P, FT, NTOK], f32r) for name in ("g_hi", "g_lo"))
            LO_DVE, LO_POOL = (0, 1, 4, 5), (2, 3)
            x1sq = sb("x1sq", [P, TPC, C])
            s6a, s6b = sb("s6a", [P, TPC, 6]), sb("s6b", [P, TPC, 6])
            mva, mvb = sb("mva", [P, TPC, 2]), sb("mvb", [P, TPC, 2])
            vea, veb = sb("vea", [P, TPC]), sb("veb", [P, TPC])
            rsa, rsb = sb("rsa", [P, TPC]), sb("rsb", [P, TPC])

            ps_h = ps("ps_h", [P, 2, 512])
            ps_g = ps("ps_g", [P, 2, 512])
            ps_r = ps("ps_r", [P, 2, 512])
            ps_o = ps("ps_o", [P, 2, 512])

            def tok(t):
                return t[:, :, 0:2 * C]

            def tok_tile(t, k):
                return t[:, k // 2, (k % 2) * C:(k % 2 + 1) * C]

            def two(t):
                return t[:, :, :].rearrange("p (a b) c -> p a (b c)", b=2)

            s_init = sem("init_done")
            s_x = [sem(f"x_loaded{b}") for b in range(2)]
            s_gs, s_gn = sem("gn_scaled"), sem("gn_done")
            s_st1, s_ag1, s_ve1 = sem("ln1_stats"), sem("ln1_aggregated"), sem("ln1_var_eps")
            s_rs1, s_xn = sem("ln1_rstd"), sem("xn_ready")
            s_t1, s_xh, s_xl = sem("xn_transposed"), sem("xn_hi_ready"), sem("xn_lo_ready")
            s_scan, s_hh, s_hl = sem("scan_summed"), sem("h_hi_ready"), sem("h_lo_ready")
            s_cm, s_res, s_rsum = sem("mixed"), sem("residual_ready"), sem("residual_summed")
            s_st2, s_ag2, s_ve2 = sem("ln2_stats"), sem("ln2_aggregated"), sem("ln2_var_eps")
            s_rs2, s_y = sem("ln2_rstd"), sem("y_ready")
            s_t2, s_yh, s_yl = sem("y_transposed"), sem("y_hi_ready"), sem("y_lo_ready")
            s_w1, s_gelu = sem("hidden_summed"), sem("hidden_ready")
            s_gh, s_gld, s_glp = sem("hidden_hi_ready"), sem("hidden_lo_ready_dve"), sem("hidden_lo_ready_pool")
            s_w2a, s_w2 = sem("mlp_first_half_summed"), sem("mlp_summed")
            s_xa, s_x1a, s_xb, s_x1 = (sem("x1_first_half_upper"), sem("x1_first_half_ready"),
                                       sem("x1_second_half_upper"), sem("x1_ready"))
            s_sq, s_acc1, s_acc2 = sem("x1_squared"), sem("x1_accumulated"), sem("x1_squares_accumulated")
            s_st = [sem(f"x1_stored{b}") for b in range(2)]
            STORES = 16 * 2 * (TPC + 3)

            def slots(engine, slot):
                for n in range(-2, 4):
                    slot(n // 2, n % 2)
                with engine.Fori(2, T - 1) as t:
                    slot(t, 0)
                    slot(t, 1)
                for n in range(STEPS - 2, STEPS + 1):
                    slot(n // 2, n % 2)

            def there(n):
                return not isinstance(n, int) or 0 <= n < STEPS

            block = ctx.enter_context(nc.Block())

            @block.sync
            def _(sp):
                def slot(t, c):
                    n = CHUNKS * t + c
                    if there(n + 2):
                        upto(sp, s_res, n + 1)
                        sp.dma_start(xt[c][:, :, :],
                                     x[TPC * c:TPC * (c + 1), :, bass.ds(t + 1, 1), :]
                                     .rearrange("k p t c -> p k (t c)")).then_inc(s_x[c], 16)
                    if there(n - 1):
                        d, u = (1 - c), (t if c else t - 1)
                        i = u // WS
                        a, b = (WS + SHIFT - 1 - i) // WS, (WS + SHIFT - 1 - u % WS) // WS
                        sp.wait_ge(s_init, 1)
                        sp.wait_ge(s_x1, n)
                        for q in range(2):
                            imgs = slice(2 * TPC * d + q, 2 * TPC * (d + 1), 2)
                            base = q * WINS
                            rows, cols = bass.ds(1 - a, CELLS), bass.ds(1 - b, CELLS)
                            row, col = bass.ds(CELLS + 1 - a, 1), bass.ds(CELLS + 1 - b, 1)
                            parts = [(x1[d][base:base + WINS, k, :],
                                      x1_cells[rows, imgs.start + 2 * k, cols, bass.ds(u, 1), :]
                                      .rearrange("r w t c -> r w (t c)")) for k in range(TPC)]
                            parts += [(x1[d][base:base + CELLS, :, :],
                                       x1_cells[row, imgs, cols, bass.ds(u, 1), :]
                                       .rearrange("r k w t c -> (r w) k (t c)")),
                                      (x1[d][base:base + WINS:CELLS, :, :],
                                       x1_cells[rows, imgs, col, bass.ds(u, 1), :]
                                       .rearrange("r k w t c -> (r w) k (t c)")),
                                      (x1[d][base:base + 1, :, :],
                                       x1_cells[row, imgs, col, bass.ds(u, 1), :]
                                       .rearrange("r k w t c -> (r w) k (t c)"))]
                            for src, dst in parts:
                                sp.dma_start(dst, src).then_inc(s_st[d], 16)

                slots(sp, slot)
                for d in range(2):
                    sp.wait_ge(s_st[d], STORES * T)

            @block.scalar
            def _(act):
                act.wait_ge(s_init, 1)

                def upper_parts(hi, full):
                    act.activation(hi[:, 0, :], full[:, 0, :], ACT.Copy)
                    return act.activation(hi[0:CB, 1, :], full[0:CB, 1, :], ACT.Copy)

                def slot(t, c):
                    n = CHUNKS * t + c
                    if there(n + 1):
                        d = 1 - c
                        act.wait_ge(s_scan, n + 2)
                        upto(act, s_cm, n)
                        for k, rows in enumerate((P, CB)):
                            last = act.activation(h_hi[d][0:rows, k, :], ps_h[0:rows, k, :], ACT.Identity,
                                                  bias=hbias[0:rows, k:k + 1])
                        last.then_inc(s_hh, 1)
                    if there(n):
                        act.wait_ge(s_t2, n + 1)
                        upper_parts(y_hi, ps_g).then_inc(s_yh, 1)
                    if there(n):
                        for f in range(FT):
                            act.wait_ge(s_w1, FT * n + f + 1)
                            if f == 0:
                                upto(act, s_w2, n)
                            elif f >= 4:
                                act.wait_ge(s_gld, len(LO_DVE) * n + LO_DVE.index(f - 4) + 1)
                            act.activation(gF[f % 4][:, :], ps_g[:, f % 2, :], ACT.Gelu,
                                           bias=b1f[:, f:f + 1]).then_inc(s_gelu, 1)
                            for g in range(max(f - 1, 0), f + (f == FT - 1)):
                                act.wait_ge(s_gelu, FT * n + g + 1)
                                act.activation(g_hi[:, g, :], gF[g % 4][:, :], ACT.Copy).then_inc(s_gh, 1)
                    if there(n + 2):
                        act.wait_ge(s_t1, n + 3)
                        upto(act, s_scan, n + 1)
                        upper_parts(xn_hi[c], ps_h).then_inc(s_xh, 1)

                slots(act, slot)

            @block.gpsimd
            def _(pool):
                for c in range(2):
                    pool.memset(h_hi[c][:, :, :].bitcast(fp32), 0.0)
                    last = pool.memset(h_lo[c][:, :].bitcast(fp32), 0.0)
                last.then_inc(s_init, 1)

                def slot(t, c):
                    n = CHUNKS * t + c
                    if there(n + 1):
                        d = 1 - c
                        pool.wait_ge(s_gs, n + 2)
                        upto(pool, s_x1, n)
                        pool.tensor_tensor(res[d][:, :, :], xt[d][:, :, :],
                                           b2b[:, :].unsqueeze(1).to_broadcast([P, TPC, C]),
                                           ALU.add).then_inc(s_res, 1)
                    if there(n + 2):
                        pool.wait_ge(s_ve1, n + 3)
                        pool.tensor_tensor(rsa[:, :], vea[:, :], neg_half[:, :], ALU.pow).then_inc(s_rs1, 1)
                    if there(n):
                        for f in LO_POOL:
                            pool.wait_ge(s_gh, FT * n + f + 1)
                            pool.tensor_tensor(g_lo[:, f, :], gF[f % 4][:, :], g_hi[:, f, :], ALU.subtract)\
                                .then_inc(s_glp, 1)
                    if there(n + 1):
                        pool.wait_ge(s_ve2, n + 2)
                        pool.tensor_tensor(rsb[:, :], veb[:, :], neg_half[:, :], ALU.pow).then_inc(s_rs2, 1)
                    if there(n - 1):
                        d = 1 - c
                        pool.wait_ge(s_x1, n)
                        upto(pool, s_acc2, n - 1)
                        upto(pool, s_acc1, n - 1)
                        pool.tensor_tensor(x1sq[:, :, :], x1[d][:, :, :], x1[d][:, :, :], ALU.mult).then_inc(s_sq, 1)
                        a = acc_x[:, TPC * d:TPC * (d + 1), :]
                        pool.tensor_tensor(a, a, x1[d][:, :, :], ALU.add).then_inc(s_acc1, 1)
                        pool.wait_ge(s_sq, n)
                        a = acc_x2[:, TPC * d:TPC * (d + 1), :]
                        pool.tensor_tensor(a, a, x1sq[:, :, :], ALU.add).then_inc(s_acc2, 1)

                slots(pool, slot)

            @block.vector
            def _(dve):
                def lower_parts(hi, lo, full, bias=None):
                    for k, rows, dst in ((0, P, lo[:, :]), (1, CB, hi[CB:P, 1, :])):
                        src, up = full[0:rows, k, :], hi[0:rows, k, :]
                        if bias is None:
                            last = dve.tensor_tensor(dst, src, up, ALU.subtract)
                        else:
                            last = dve.scalar_tensor_tensor(out=dst, in0=src, scalar=bias[0:rows, k:k + 1], in1=up,
                                                            op0=ALU.add, op1=ALU.subtract)
                    return last

                def x1_half(b, half, partial, count):
                    tiles = slice(2 * half, 2 * half + 2)
                    dve.tensor_tensor(x1[b][:, tiles, :], ps_o[:, :, 0:C], res[b][:, tiles, :],
                                      ALU.add).then_inc(partial, 1)
                    dve.wait_ge(partial, count)
                    return dve.tensor_tensor(x1[b][:, tiles, :], ps_o[:, :, C:2 * C], x1[b][:, tiles, :], ALU.add)

                def slot(t, c):
                    n = CHUNKS * t + c
                    if there(n + 2):
                        dve.wait_ge(s_x[c], 16 * (t + 2))
                        upto(dve, s_t1, n + 1)
                        r = slice(TPC * c, TPC * (c + 1))
                        dve.tensor_tensor(xn[c][:, :, :], xt[c][:, :, :], R1[:, r, :], ALU.mult).then_inc(s_gs, 1)
                        dve.wait_ge(s_gs, n + 3)
                        dve.tensor_tensor(xn[c][:, :, :], xn[c][:, :, :], M1[:, r, :],
                                          ALU.subtract).then_inc(s_gn, 1)
                    if there(n + 1):
                        dve.wait_ge(s_hh, n + 2)
                        lower_parts(h_hi[1 - c], h_lo[1 - c], ps_h, hbias).then_inc(s_hl, 1)
                    if there(n):
                        dve.wait_ge(s_yh, n + 1)
                        lower_parts(y_hi, y_lo, ps_g).then_inc(s_yl, 1)
                    if there(n - 1):
                        dve.wait_ge(s_w2, n)
                        x1_half(1 - c, 1, s_xb, n).then_inc(s_x1, 1)
                    if there(n + 2):
                        dve.wait_ge(s_gn, n + 3)
                        for k in range(TPC):
                            last = dve.bn_stats(s6a[:, k, :], xn[c][:, k, :])
                        last.then_inc(s_st1, 1)
                        dve.wait_ge(s_w, 16 * WEIGHT_LOADS)
                        dve.wait_ge(s_st1, n + 3)
                        for k in range(TPC):
                            last = dve.bn_aggr(mva[:, k, :], s6a[:, k, :])
                        last.then_inc(s_ag1, 1)
                        dve.wait_ge(s_ag1, n + 3)
                        dve.tensor_scalar(vea[:, :], mva[:, :, 1], LN_EPS, None, ALU.add).then_inc(s_ve1, 1)
                    if there(n):
                        for f in LO_DVE[:2]:
                            dve.wait_ge(s_gh, FT * n + f + 1)
                            dve.tensor_tensor(g_lo[:, f, :], gF[f % 4][:, :], g_hi[:, f, :], ALU.subtract)\
                                .then_inc(s_gld, 1)
                    if there(n + 2):
                        dve.wait_ge(s_rs1, n + 3)
                        for k in range(TPC):
                            last = dve.tensor_scalar(xn[c][:, k, :], xn[c][:, k, :], mva[:, k, 0:1], rsa[:, k:k + 1],
                                                     ALU.subtract, ALU.mult)
                        last.then_inc(s_xn, 1)
                    if there(n):
                        for f in LO_DVE[2:]:
                            dve.wait_ge(s_gh, FT * n + f + 1)
                            dve.tensor_tensor(g_lo[:, f, :], gF[f % 4][:, :], g_hi[:, f, :], ALU.subtract)\
                                .then_inc(s_gld, 1)
                    if there(n + 1):
                        d = 1 - c
                        dve.wait_ge(s_cm, n + 2)
                        for k in range(TPC):
                            last = dve.bn_stats(s6b[:, k, :], tok_tile(ps_r, k))
                        last.then_inc(s_st2, 1)
                        dve.wait_ge(s_w, 16 * WEIGHT_LOADS)
                        dve.wait_ge(s_st2, n + 2)
                        for k in range(TPC):
                            last = dve.bn_aggr(mvb[:, k, :], s6b[:, k, :])
                        last.then_inc(s_ag2, 1)
                        dve.wait_ge(s_ag2, n + 2)
                        dve.tensor_scalar(veb[:, :], mvb[:, :, 1], LN_EPS, None, ALU.add).then_inc(s_ve2, 1)
                    if there(n + 2):
                        dve.wait_ge(s_xh, n + 3)
                        lower_parts(xn_hi[c], xn_lo[c], ps_h).then_inc(s_xl, 1)
                    if there(n + 1):
                        d = 1 - c
                        dve.wait_ge(s_res, n + 2)
                        dve.tensor_tensor(two(res[d]), tok(ps_r), two(res[d]), ALU.add).then_inc(s_rsum, 1)
                        dve.wait_ge(s_rs2, n + 2)
                        upto(dve, s_t2, n + 1)
                        for k in range(TPC):
                            last = dve.tensor_scalar(yb[:, k, :], tok_tile(ps_r, k), mvb[:, k, 0:1], rsb[:, k:k + 1],
                                                     ALU.subtract, ALU.mult)
                        last.then_inc(s_y, 1)

                    if there(n):
                        dve.wait_ge(s_w2a, n + 1)
                        if not isinstance(n, int) or n >= 2:
                            dve.wait_ge(s_acc2, n - 1)
                            dve.wait_ge(s_st[c], STORES * t)
                        x1_half(c, 0, s_xa, n + 1).then_inc(s_x1a, 1)

                slots(dve, slot)

            @block.tensor
            def _(pe):
                pe.wait_ge(s_init, 1)

                def transposes(dst, src):
                    for k in range(TPC):
                        pe.transpose(dst[:, 0, P * k:P * (k + 1)], src[:, k, 0:P], ident[:, :])
                    for k in range(TPC):
                        last = pe.transpose(dst[0:CB, 1, P * k:P * (k + 1)], src[:, k, P:C], ident[:, :])
                    return last

                def second_layer(half):
                    for k in (2 * half, 2 * half + 1):
                        for f in range(FT):
                            both = (ps_o[:, k % 2, 0:2 * C], g_hi, w2[:, f, :, :].rearrange("p a c -> p (a c)"))
                            upper = (ps_o[:, k % 2, 0:C], g_lo, w2[:, f, 0, :])
                            terms = (upper, both) if f == FT - 1 else (both, upper)
                            for i, (dst, g, w) in enumerate(terms):
                                last = pe.matmul(dst, g[:, f, P * k:P * (k + 1)], w,
                                                 start=(f == 0 and i == 0), stop=(f == FT - 1 and i == 1))
                    return last

                def slot(t, c):
                    n = CHUNKS * t + c
                    if there(n + 1):
                        d = 1 - c
                        pe.wait_ge(s_xl, n + 2)
                        upto(pe, s_hl, n)
                        for m, rows in enumerate((P, CB)):
                            cols = slice(P * m, P * m + rows)
                            terms = (*W_B.terms(xn_hi[d], xn_lo[d], cols), *W_A.terms(h_hi[d], h_lo[d], cols))
                            for k, (w, v) in enumerate(terms):
                                last = pe.matmul(ps_h[0:rows, m, :], w, v, start=(k == 0), stop=(k == len(terms) - 1))
                        last.then_inc(s_scan, 1)
                    if there(n):
                        pe.wait_ge(s_y, n + 1)
                        upto(pe, s_gelu, FT * n)
                        transposes(ps_g, yb).then_inc(s_t2, 1)
                    if there(n - 1):
                        pe.wait_ge(s_x1a, n)
                        second_layer(1).then_inc(s_w2, 1)
                    if there(n):
                        pe.wait_ge(s_yl, n + 1)
                        for f in range(FT):
                            if f >= 2:
                                pe.wait_ge(s_gelu, FT * n + f - 1)
                            terms = W_1.terms(y_hi, y_lo, slice(P * f, P * (f + 1)))
                            for k, (w, v) in enumerate(terms):
                                last = pe.matmul(ps_g[:, f % 2, :], w, v, start=(k == 0), stop=(k == len(terms) - 1))
                            last.then_inc(s_w1, 1)
                    if there(n + 1):
                        d = 1 - c
                        pe.wait_ge(s_hl, n + 2)
                        upto(pe, s_y, n + 1)
                        upto(pe, s_rsum, n + 1)
                        for k in range(TPC):
                            terms = W_C.terms(h_hi[d], h_lo[d], slice(0, C), lambda v: v[:, P * k:P * (k + 1)])
                            for i, (w, v) in enumerate(terms):
                                last = pe.matmul(tok_tile(ps_r, k), v, w, start=(i == 0), stop=(i == len(terms) - 1))
                        last.then_inc(s_cm, 1)
                    if there(n + 2):
                        pe.wait_ge(s_xn, n + 3)
                        upto(pe, s_hl, n + 2)
                        transposes(ps_h, xn[c]).then_inc(s_t1, 1)
                    if there(n):
                        upto(pe, s_x1, n)
                        pe.wait_ge(s_gld, len(LO_DVE) * (n + 1))
                        pe.wait_ge(s_glp, len(LO_POOL) * (n + 1))
                        second_layer(0).then_inc(s_w2a, 1)

                slots(pe, slot)

        bias_tab = [[top.enter_context(nc.sbuf_tensor(f"bias_{r}{k}", [P, HEADS, T], fp32)) for k in range(2)]
                    for r in range(2)]
        with ExitStack() as ctx:
            def sb(name, shape, dt=fp32):
                return ctx.enter_context(nc.sbuf_tensor(name, shape, dt))

            def ps(name, shape):
                return ctx.enter_context(nc.psum_tensor(name, shape, fp32))

            NG = NT * GROUPS
            RPB = (2 * WS - 1) ** 2
            hot0, hot1 = sb("hot0", [P, T, T]), sb("hot1", [RPB - P, T, T])
            tab0, tab1 = sb("tab0", [P, HEADS]), sb("tab1", [RPB - P, HEADS])
            mask = sb("mask", [P, 4, T])
            pm2 = sb("pm2", [P, 2, NG])
            mean2, var2 = (sb(f"{w}2", [P, 2, 2]) for w in ("mean", "var"))
            tab2 = sb("tab2", [P, 2, 2, 2])
            row2 = sb("row2", [P, 8, CG])
            base = sb("base", [P, HEADS, T])
            MB = 512 // HEADS
            s_l = sem("tables_loaded")
            s_v2, s_p2, s_m2, s_s2 = sem("gn2_steps"), sem("gn2_rstd"), sem("gn2_sums"), sem("gn2_stored")
            s_b2 = sem("bias_gathered")

            UW = UP * P
            NW = 2 * UP
            TE = T + T % 2
            PA = P // (2 * HD)
            JB = JP // 2
            W_QKV = Split(ctx, "wqkv", 3 * C)
            raw = sb("raw_qkv", [P, 2, 3 * C])
            wp = sb("wp", [P, 2, C])
            bqkv = sb("bqkv", [P, 5])
            hm = sb("hm", [P, 2])
            bkm = sb("bkm", [P, 2, 2])
            pbb = sb("pbb", [P, C])
            xb = [sb(f"xb{b}", [P, UP, C]) for b in range(2)]
            gnr = [sb(f"gnr{b}", [P, 2 * C]) for b in range(2)]
            xn = sb("xn_u", [P, UP, C])
            rs = [sb(f"rs{b}", [P, UP, C]) for b in range(2)]
            yo = [sb(f"yo{b}", [P, UP, C]) for b in range(2)]
            x_hi, x_lo = sb("x_hi", [P, 2, UW], f32r), sb("x_lo", [P, UW], f32r)
            Qm = [sb(f"Qm{b}", [P, JP, NW, SLOT]) for b in range(2)]
            Kp = [sb(f"Kp{b}", [P, 2, 2, NW, T]) for b in range(2)]
            Vx = [sb(f"Vx{b}", [P, NW, JP, 2 * HD]) for b in range(2)]
            L = [sb(f"L{b}", [P, HEADS, T]) for b in range(UP)]
            E = [sb(f"E{b}", [P, HEADS, SLOT]) for b in range(UP)]
            mx = [sb(f"mx{b}", [P, HEADS]) for b in range(UP)]
            sm = [sb(f"sm{b}", [P, HEADS]) for b in range(UP)]
            ri = [sb(f"ri{b}", [P, HEADS]) for b in range(UP)]
            PT = [sb(f"PT{b}", [P, JP, P]) for b in range(2)]
            oT = [[sb(f"oT{b}{p}", [P, 2, 2, SLOT]) for p in range(UP)] for b in range(2)]
            ps_s = ps("ps_s", [P, 2, 512])
            ps_t = ps("ps_t", [P, 2, 512])
            ps_v = ps("ps_v", [P, 512])
            OUT0, TURN, QK, VAL, OUT1 = 0, 1, 3, 6, 8
            banks = [ps(f"ps_w{b}", [P, 512]) for b in range(3)]

            def ps_w(task):
                return banks[task % 3]

            ps_m, ps_b = banks[0], ps_s

            s_w3, s_i3 = sem("attention_weights_loaded"), sem("attention_init")
            s_pad, s_xpad, s_tabs = sem("attention_pads_set"), sem("token_pads_set"), sem("tables_done")
            s_xb = [sem(f"unit_loaded{b}") for b in range(2)]
            s_ns, s_nx = sem("unit_scaled"), sem("unit_normed")
            s_tx, s_xh, s_xl = sem("unit_transposed"), sem("unit_upper_parts"), sem("unit_lower_parts")
            s_ws3 = sem("attention_weights_upper_parts")
            s_qk, s_qkm, s_qb = sem("queries_keys_summed"), sem("queries_keys_masked"), sem("queries_b_masked")
            s_v, s_vx = sem("v_summed"), [sem(f"v_spread{half}") for half in range(2)]
            s_sc, s_lg, s_mx, s_sub = sem("scores_summed"), sem("logits"), sem("row_maxima"), sem("maxima_off")
            s_ex, s_sm, s_ri, s_nm = sem("exponentials"), sem("row_sums"), sem("row_reciprocals"), sem("probabilities")
            s_pt, s_ptc = sem("probs_transposed"), sem("probs_copied")
            s_pv, s_o = sem("values_summed"), sem("heads_ready")
            s_pj, s_yo = sem("projected"), sem("unit_out_ready")
            s_rs = sem("unit_residual")
            s_so = [sem(f"unit_stored{b}") for b in range(2)]
            LOADS = 2 + 1
            WEIGHT_LOADS3 = 6
            block = ctx.enter_context(nc.Block())

            def units(engine, slot):
                last_row = IMGS * (CELLS - 1)
                for u in range(-2, 4):
                    slot(u // 2, u % 2, 0)
                with engine.Fori(2, last_row // 2) as i:
                    slot(i, 0, 0)
                    slot(i, 1, 0)
                with engine.Fori(last_row // 2, UNITS // 2 - 1) as i:
                    slot(i, 0, 1)
                    slot(i, 1, 1)
                for u in (UNITS - 2, UNITS - 1, UNITS):
                    slot(u // 2, u % 2, 1)

            def is_unit(u):
                return not isinstance(u, int) or 0 <= u < UNITS

            def lagged(u, c, p):
                return (u, c, p - 2) if p >= 2 else (u - 1, 1 - c, p + 2)

            def spread(copy, c, half):
                for w in range(2):
                    for e in range(2):
                        src = ps_w(VAL + half)[SLOT * w:SLOT * (w + 1), 0:2 * C]\
                            .rearrange("p (a j e) -> p a j e", a=2, j=JP)[:, :, :, HD * e:HD * (e + 1)]
                        last = copy(Vx[1 - c][SLOT * e:SLOT * (e + 1), 4 * half + w:4 * half + w + 3:2, :,
                                              HD * e:HD * (e + 1)], src)
                return last

            @block.sync
            def _(sp):
                for dst, src in ((hot0[:, :, :], onehot[0:P]), (hot1[:, :, :], onehot[P:RPB]),
                                 (tab0[:, :], rpb[0:P]), (tab1[:, :], rpb[P:RPB]), (mask[:, :, :], shift_mask)):
                    sp.dma_start(dst, src).then_inc(s_l, 16)
                for dst, src in ((raw[:, :, :], qkvT.rearrange("(k p) n -> p k n", p=P)),
                                 (wp[:, 0, :], projT[0:P]), (wp[0:CB, 1, :], projT[P:C]),
                                 (bqkv[:, :], qkv_b),
                                 (hm[:, :], head_masks), (pbb[:, :], proj_b.partition_broadcast(P))):
                    sp.dma_start(dst, src).then_inc(s_w3, 16)
                sp.wait_ge(s_v2, 7)
                for a in range(2):
                    for h in range(2):
                        for q in range(2):
                            sp.dma_start(gn2_rows[2 * TH * h + q:2 * TH * (h + 1):2, a, :]
                                         .rearrange("k (g e) -> k g e", e=CG),
                                         row2[:, 4 * a + 2 * h + q, :]).then_inc(s_s2, 16)
                sp.wait_ge(s_s2, 16 * 8)
                sp.wait_ge(s_xpad, 1)

                x1_rows = x1_cells.rearrange("r k w t c -> (r k) w t c")

                def load(i, c):
                    u = 2 * i + c
                    for w in range(2):
                        src = x1_rows[bass.ds(u + IMGS, 1), w + 1:w + 2 * UP:2, :, :].rearrange("u w t c -> (u t) w c")
                        sp.dma_start(xb[c][SLOT * w:SLOT * w + T, :, :], src).then_inc(s_xb[c], 16)
                    sp.dma_start(gnr[c][:, :], gn2_rows[bass.ds(u % IMGS, 1), :, :]
                                 .rearrange("u a c -> (u a c)").partition_broadcast(P))\
                      .then_inc(s_xb[c], 16)

                def slot(i, c, r):
                    u = 2 * i + c
                    if is_unit(u + 2):
                        upto(sp, s_rs, u + 1)
                        upto(sp, s_nx, u + 1)
                        load(i + 1, c)
                    if is_unit(u - 1):
                        d = 1 - c
                        sp.wait_ge(s_yo, 2 * u)
                        for w in range(2):
                            src = yo[d][SLOT * w:SLOT * w + T, :, :]
                            sp.dma_start(out[bass.ds(u - 1, 1), :, w, :, :].rearrange("u p t c -> (u t) p c"), src)\
                              .then_inc(s_so[d], 16)

                units(sp, slot)
                for d in range(2):
                    sp.wait_ge(s_so[d], 32 * UNITS // 2)

            @block.gpsimd
            def _(pool):
                pool.memset(xb[0][:, :, :], 0.0)
                pool.memset(xb[1][:, :, :], 0.0).then_inc(s_xpad, 1)
                pool.wait_ge(s_v2, 5)
                pool.tensor_tensor(tab2[:, 0, :, :], var2[:, :, :],
                                   neg_half[:, :].rearrange("p (a b) -> p a b", a=2), ALU.pow).then_inc(s_p2, 1)
                pool.memset(Qm[0][:, :, :, :], 0.0)
                pool.memset(Kp[0][:, :, :, :, :], 0.0)
                for b in range(2):
                    for p in range(UP):
                        pool.memset(oT[b][p][:, :, :, :], 0.0)
                pool.memset(rs[0][:, :, :], 0.0).then_inc(s_pad, 1)
                pool.wait_ge(s_w3, 16 * WEIGHT_LOADS3)
                pool.wait_ge(s_ws3, 1)
                for t in range(2):
                    last = pool.tensor_tensor(W_QKV.parts[2 * t + 1][:, :], raw[:, t, :], W_QKV.parts[2 * t][:, :],
                                              ALU.subtract)
                last.then_inc(s_pad, 1)

                def norm(u, p):
                    k = UP * u + p
                    pool.wait_ge(s_ri, k + 1)
                    e = E[p][:, :, 0:T]
                    pool.tensor_tensor(e, e, ri[p][:, :].unsqueeze(2).to_broadcast([P, HEADS, T]), ALU.mult)\
                        .then_inc(s_nm, 1)

                def slot(i, c, r):
                    u = 2 * i + c
                    for p in range(UP):
                        pu, pp = (u, p - 1) if p else (u - 1, UP - 1)
                        if is_unit(pu):
                            norm(pu, pp)
                        if is_unit(u) and p == 0:
                            pool.wait_ge(s_xb[c], 16 * LOADS * (i + 1))
                            upto(pool, s_yo, 2 * (u - 1))
                            pool.tensor_tensor(rs[c][:, :, :], xb[c][:, :, :],
                                               pbb[:, :].unsqueeze(1).to_broadcast([P, UP, C]), ALU.add)\
                                .then_inc(s_rs, 1)
                        if is_unit(u + 2) and p >= 2:
                            if p == 2:
                                pool.wait_ge(s_xb[c], 16 * LOADS * (i + 2))
                                upto(pool, s_tx, 2 * (u + 2))
                                pool.tensor_tensor(xn[:, :, :], xb[c][:, :, :],
                                                   gnr[c][:, 0:C].unsqueeze(1).to_broadcast([P, UP, C]), ALU.mult)\
                                    .then_inc(s_ns, 1)
                            else:
                                pool.wait_ge(s_ns, u + 3)
                                pool.tensor_tensor(xn[:, :, :], xn[:, :, :],
                                                   gnr[c][:, C:2 * C].unsqueeze(1).to_broadcast([P, UP, C]), ALU.subtract)\
                                    .then_inc(s_nx, 1)

                units(pool, slot)

            @block.scalar
            def _(act):
                act.wait_ge(s_w3, 16 * WEIGHT_LOADS3)
                for t in range(2):
                    last = act.activation(W_QKV.parts[2 * t][:, :], raw[:, t, :], ACT.Copy)
                last.then_inc(s_ws3, 1)
                act.wait_ge(s_i3, 2)
                act.wait_ge(s_pad, 1)

                def upper(i, c, h):
                    v, rows = 2 * i + c + 1, slice(CB * h, P)
                    act.wait_ge(s_tx, 2 * v + h + 1)
                    if h == 0:
                        upto(act, s_v, 2 * v)
                    act.activation(x_hi[rows, h, :], ps_w(TURN + h)[rows, :], ACT.Copy).then_inc(s_xh, 1)

                def masked(i, c, m):
                    v, d = 2 * i + c + 1, 1 - c
                    full = ps_w(QK + m)[:, 0:NW * TE].rearrange("p (w t) -> p w t", t=TE)[:, :, 0:T]
                    act.wait_ge(s_qk, 3 * v + m + 1)
                    if m == 0:
                        upto(act, s_sc, UP * (v - 1))
                        for j in range(PA):
                            rows = slice(2 * HD * j, 2 * HD * (j + 1))
                            last = act.activation(Qm[d][rows, j, :, 0:T], full[rows], ACT.Identity,
                                                  bias=bqkv[rows, 0:1])
                    else:
                        rows, k = (CB, 1) if m == 1 else (P, 0)
                        for e in range(2):
                            last = act.activation(Kp[d][0:rows, k, e, :, :], full[0:rows], ACT.Identity,
                                                  scale=hm[0:rows, e:e + 1], bias=bkm[0:rows, e, k:k + 1])
                    last.then_inc(s_qkm, 1)

                def slot(i, c, r):
                    u = 2 * i + c
                    nxt = is_unit(u + 1)
                    for p in range(UP):
                        pu, pp = (u, p - 1) if p else (u - 1, UP - 1)
                        if is_unit(pu):
                            k = UP * u + p - 1
                            act.wait_ge(s_sub, k + 1)
                            upto(act, s_pt, k - 3)
                            act.activation(E[pp][:, :, 0:T], L[pp][:, :, :], ACT.Exp).then_inc(s_ex, 1)
                        if nxt and p == 2:
                            masked(i, c, 1)
                        lu, lc, lp = lagged(u, c, p)
                        k = UP * u + p - 2
                        if is_unit(lu):
                            act.wait_ge(s_pt, k + 1)
                            upto(act, s_pv, k - 1)
                            act.activation(PT[lp % 2][:, :, :].rearrange("p (a b) q -> p a (b q)", a=2),
                                           ps_t[:, :, 0:JB * P], ACT.Copy).then_inc(s_ptc, 1)
                        if nxt and p == 1:
                            masked(i, c, 0)
                        if nxt and p == 2:
                            masked(i, c, 2)
                        if nxt and p == 3:
                            act.wait_ge(s_v, 2 * (u + 1) + 2)
                            upto(act, s_pv, UP * u)
                            spread(lambda out, src: act.activation(out, src, ACT.Copy), c, 1).then_inc(s_vx[1], 1)
                        if nxt and p == 0:
                            upper(i, c, 0)
                        if is_unit(lu):
                            act.wait_ge(s_pv, k + 1)
                            upto(act, s_pj, 2 * (lu - 1))
                            for h, rows in enumerate((P, CB)):
                                src = ps_v[0:rows, h * P:(h + 1) * P].rearrange("p (w t) -> p w t", w=2)
                                last = act.activation(oT[lc][lp][0:rows, h, :, 0:T], src[:, :, 0:T], ACT.Identity,
                                                      bias=bqkv[0:rows, 3 + h:4 + h])
                            last.then_inc(s_o, 1)
                        if nxt and p == 0:
                            upper(i, c, 1)

                units(act, slot)

            @block.vector
            def _(dve):
                done = [0]

                def link(ins):
                    done[0] += 1
                    ins.then_inc(s_v2, 1)
                    dve.wait_ge(s_v2, done[0])

                for k, acc in enumerate((acc_x, acc_x2)):
                    last = dve.tensor_reduce(pm2[:, k, :], acc[:, :, :].rearrange("p k (g e) -> p (k g) e", e=CG),
                                             AX.X, ALU.add)
                link(last)
                dve.wait_ge(s_m2, 1)
                per = 1.0 / (T * CG)
                sums = ps_m[:, 0:8].rearrange("p (a h q) -> p a h q", a=2, h=2)
                link(dve.tensor_scalar(mean2[:, :, :], sums[:, 0], per, None, ALU.mult))
                link(dve.tensor_tensor(tab2[:, 1, :, :], mean2[:, :, :], mean2[:, :, :], ALU.mult))
                link(dve.scalar_tensor_tensor(out=var2[:, :, :], in0=sums[:, 1], scalar=per,
                                              in1=tab2[:, 1, :, :], op0=ALU.mult, op1=ALU.subtract))
                link(dve.tensor_scalar(var2[:, :, :], var2[:, :, :], GN_EPS, None, ALU.add))
                dve.wait_ge(s_p2, 1)
                link(dve.tensor_tensor(tab2[:, 1, :, :], mean2[:, :, :], tab2[:, 0, :, :], ALU.mult))
                link(dve.tensor_copy(row2[:, :, :], tab2[:, :, :, :].rearrange("p a h q -> p (a h q)")
                                     .unsqueeze(2).to_broadcast([P, 8, CG])))
                link(dve.memset(base[:, :, :], 0.0))
                dve.memset(Qm[1][:, :, :, :], 0.0)
                dve.memset(Kp[1][:, :, :, :, :], 0.0)
                dve.memset(wp[CB:P, 1, :], 0.0)
                for b in range(2):
                    dve.memset(Vx[b][:, :, :, :], 0.0)
                for p in range(UP):
                    last = dve.memset(E[p][:, :, :], 0.0)
                last.then_inc(s_i3, 1)
                dve.wait_ge(s_b2, 1)
                for w in range(2):
                    for b in range(2):
                        m0, m1 = MB * b, min(MB * (b + 1), T)
                        last = dve.tensor_copy(base[SLOT * w:SLOT * w + T, :, m0:m1],
                                               ps_b[0:T, b, 0:(m1 - m0) * HEADS].rearrange("p (m h) -> p h m", h=HEADS))
                link(last)
                for r in range(2):
                    for k in range(2):
                        last = dve.tensor_tensor(bias_tab[r][k][:, :, :], base[:, :, :],
                                                 mask[:, 2 * r + k, :].unsqueeze(1).to_broadcast([P, HEADS, T]), ALU.add)
                last.then_inc(s_tabs, 1)
                dve.wait_ge(s_tabs, 1)
                dve.wait_ge(s_w3, 16 * WEIGHT_LOADS3)
                for k, column in ((0, 2), (1, 1)):
                    last = dve.tensor_scalar(bkm[:, :, k], hm[:, :], bqkv[:, column:column + 1], None, ALU.mult)
                last.then_inc(s_i3, 1)
                dve.wait_ge(s_i3, 2)

                def lower(i, c, h):
                    v, rows = 2 * i + c + 1, slice(CB * h, P)
                    dve.wait_ge(s_xh, 2 * v + h + 1)
                    dst = x_lo[:, :] if h == 0 else x_hi[0:CB, 1, :]
                    dve.tensor_tensor(dst, ps_w(TURN + h)[rows, :], x_hi[rows, h, :],
                                      ALU.subtract).then_inc(s_xl, 1)

                def queries_b(i, c):
                    v = 2 * i + c + 1
                    full = ps_w(QK + 1)[:, 0:NW * TE].rearrange("p (w t) -> p w t", t=TE)[:, :, 0:T]
                    dve.wait_ge(s_qk, 3 * v + 2)
                    upto(dve, s_sc, UP * (v - 1))
                    for j in range(PA, JP):
                        src, dst = CB + 2 * HD * (j - PA), 2 * HD * (j - PA)
                        last = dve.tensor_scalar(Qm[1 - c][dst:dst + 2 * HD, j, :, 0:T], full[src:src + 2 * HD],
                                                 bqkv[src:src + 2 * HD, 1:2], None, ALU.add)
                    last.then_inc(s_qb, 1)

                def finish(i, c, half):
                    v, d = 2 * i + c - 1, 1 - c
                    dve.wait_ge(s_pj, 2 * v + half + 1)
                    if half == 0:
                        dve.wait_ge(s_rs, v + 1)
                        upto(dve, s_so[d], 32 * (i if c else i - 1))
                    ab = slice(2 * half, 2 * half + 2)
                    full = ps_w(OUT1 if half else OUT0)[:, 0:2 * C].rearrange("p (a c) -> p a c", a=2)
                    dve.tensor_tensor(yo[d][:, ab, :], full, rs[d][:, ab, :], ALU.add).then_inc(s_yo, 1)

                def slot(i, c, r):
                    u = 2 * i + c
                    nxt = is_unit(u + 1)
                    for p in range(UP):
                        k = UP * u + p
                        pu, pp = (u, p - 1) if p else (u - 1, UP - 1)
                        if is_unit(u):
                            dve.wait_ge(s_sc, k + 1)
                            tab = bias_tab[r][p // (UP - 1)][:, :, :].rearrange("p (a h) m -> p a (h m)", a=2)
                            dve.scalar_tensor_tensor(out=L[p][:, :, :].rearrange("p (a h) m -> p a (h m)", a=2),
                                                     in0=ps_s[:, :, 0:HEADS // 2 * T], scalar=HD ** -0.5,
                                                     in1=tab, op0=ALU.mult, op1=ALU.add).then_inc(s_lg, 1)
                            dve.wait_ge(s_lg, k + 1)
                            dve.tensor_reduce(mx[p][:, :], L[p][:, :, :], AX.X, ALU.max).then_inc(s_mx, 1)
                        if is_unit(pu):
                            dve.wait_ge(s_ex, k)
                            dve.tensor_reduce(sm[pp][:, :], E[pp][:, :, 0:T], AX.X, ALU.add).then_inc(s_sm, 1)
                            dve.wait_ge(s_sm, k)
                            dve.reciprocal(ri[pp][:, :], sm[pp][:, :]).then_inc(s_ri, 1)
                        if is_unit(u):
                            dve.wait_ge(s_mx, k + 1)
                            dve.tensor_tensor(L[p][:, :, :], L[p][:, :, :],
                                              mx[p][:, :].unsqueeze(2).to_broadcast([P, HEADS, T]),
                                              ALU.subtract).then_inc(s_sub, 1)
                        if is_unit(u - 1) and p == 0:
                            finish(i, c, 0)
                        if nxt and p == 0:
                            lower(i, c, 0)
                            lower(i, c, 1)
                        if nxt and p == 1:
                            queries_b(i, c)
                        if nxt and p == 2:
                            dve.wait_ge(s_v, 2 * (u + 1) + 1)
                            upto(dve, s_pv, UP * u)
                            spread(dve.tensor_copy, c, 0).then_inc(s_vx[0], 1)
                        if is_unit(u - 1) and p == 3:
                            finish(i, c, 1)

                units(dve, slot)

            @block.tensor
            def _(pe):
                pe.wait_ge(s_v2, 1)
                for a in range(2):
                    for h in range(2):
                        last = pe.matmul(ps_m[:, 4 * a + 2 * h:4 * a + 2 * h + 2], pm2[:, a, P * h:P * (h + 1)],
                                         img_mean[:, :], start=True, stop=True)
                last.then_inc(s_m2, 1)
                pe.wait_ge(s_l, 16 * 5)
                for m in range(T):
                    dst = ps_b[0:T, m // MB, (m % MB) * HEADS:(m % MB + 1) * HEADS]
                    pe.matmul(dst, hot0[:, m, :], tab0[:, :], start=True, stop=False)
                    last = pe.matmul(dst, hot1[:, m, :], tab1[:, :], start=False, stop=True)
                last.then_inc(s_b2, 1)
                pe.wait_ge(s_w3, 16 * WEIGHT_LOADS3)
                pe.wait_ge(s_i3, 2)
                pe.wait_ge(s_tabs, 1)
                pe.wait_ge(s_pad, 2)

                def turn(i, c, h):
                    v = 2 * i + c + 1
                    if h == 0:
                        pe.wait_ge(s_nx, v + 1)
                        upto(pe, s_vx[1], v)
                    else:
                        upto(pe, s_yo, 2 * (v - 2))
                    for p in range(UP):
                        last = pe.transpose(ps_w(TURN + h)[:, P * p:P * (p + 1)],
                                            xn[:, p, CB * h:CB * h + P], ident[:, :])
                    last.then_inc(s_tx, 1)

                def project(i, c, m):
                    v = 2 * i + c + 1
                    if m == 0:
                        pe.wait_ge(s_xl, 2 * v + 2)
                        upto(pe, s_yo, 2 * (v - 2) + 1)
                    terms = W_QKV.terms(x_hi, x_lo, slice(P * m, P * (m + 1)),
                                        lambda a: a.rearrange("p (w t) -> p w t", t=SLOT)[:, :, 0:TE])
                    for k, (w, x) in enumerate(terms):
                        last = pe.matmul(ps_w(QK + m)[:, 0:NW * TE].rearrange("p (w t) -> p w t", t=TE), w, x,
                                         start=(k == 0), stop=(k == len(terms) - 1))
                    last.then_inc(s_qk, 1)

                def values(i, c, half):
                    v = 2 * i + c + 1
                    pe.wait_ge(s_qkm, 3 * v + half + 1)
                    if half == 1:
                        pe.wait_ge(s_qb, v + 1)
                    for a in range(2):
                        p = 2 * half + a
                        terms = W_QKV.terms(x_hi, x_lo, slice(2 * C, 3 * C), lambda t: t[:, P * p:P * (p + 1)])
                        for k, (w, x) in enumerate(terms):
                            last = pe.matmul(ps_w(VAL + half)[:, C * a:C * (a + 1)], x, w,
                                             start=(k == 0), stop=(k == len(terms) - 1))
                    last.then_inc(s_v, 1)

                def mix(i, c, half):
                    v, d = 2 * i + c - 1, 1 - c
                    pe.wait_ge(s_o, UP * v + 2 * half + 2)
                    if not is_unit(v + 2):
                        pe.wait_ge(s_vx[0], UNITS)
                        pe.wait_ge(s_yo, 2 * v)
                    elif half == 0:
                        pe.wait_ge(s_vx[0], v + 2)
                    else:
                        pe.wait_ge(s_qkm, 3 * (v + 2) + 3)
                    for a in range(2):
                        p = 2 * half + a
                        for k in range(2):
                            last = pe.matmul(ps_w(OUT1 if half else OUT0)[:, C * a:C * (a + 1)],
                                             oT[d][p][:, k, :, :].rearrange("p w t -> p (w t)"),
                                             wp[:, k, :], start=(k == 0), stop=(k == 1))
                    last.then_inc(s_pj, 1)

                def slot(i, c, r):
                    u = 2 * i + c
                    v = u + 1
                    nxt = is_unit(v)
                    for p in range(UP):
                        lu, lc, lp = lagged(u, c, p)
                        if is_unit(u):
                            k = UP * u + p
                            if p == 0:
                                pe.wait_ge(s_qkm, 3 * u + 3)
                                pe.wait_ge(s_qb, u + 1)
                            upto(pe, s_lg, k)
                            for w in range(2):
                                for j in range(JP):
                                    last = pe.matmul(ps_s[SLOT * w:SLOT * (w + 1), j // JB,
                                                          2 * T * (j % JB):2 * T * (j % JB + 1)],
                                                     Qm[c][:, j, 2 * p + w, :],
                                                     Kp[c][:, j // PA, :, 2 * p + w, :], start=True, stop=True)
                            last.then_inc(s_sc, 1)
                        if is_unit(lu):
                            k = UP * u + p - 2
                            pe.wait_ge(s_nm, k + 1)
                            upto(pe, s_ptc, k)
                            for j in range(JP):
                                last = pe.transpose(ps_t[:, j // JB, P * (j % JB):P * (j % JB + 1)],
                                                    E[lp][:, 2 * j:2 * j + 2, :].rearrange("p h m -> p (h m)"),
                                                    ident[:, :])
                            last.then_inc(s_pt, 1)
                        if is_unit(u - 1) and p == 0:
                            mix(i, c, 0)
                        if nxt:
                            if p == 1:
                                project(i, c, 0)
                            if p == 2:
                                project(i, c, 2)
                            if p == 3:
                                values(i, c, 1)
                        if nxt and p == 0:
                            turn(i, c, 0)
                        if nxt and p == 1:
                            project(i, c, 1)
                        if nxt and p == 2:
                            values(i, c, 0)
                        if is_unit(lu):
                            k = UP * u + p - 2
                            pe.wait_ge(s_ptc, k + 1)
                            pe.wait_ge(s_vx[lp // 2], lu + 1)
                            upto(pe, s_o, k)
                            for w in range(2):
                                for j in range(JP):
                                    row, col = 2 * HD * (j % PA), P * (j // PA) + SLOT * w
                                    last = pe.matmul(ps_v[row:row + 2 * HD, col:col + T],
                                                     Vx[lc][:, 2 * lp + w, j, :],
                                                     PT[lp % 2][:, j, SLOT * w:SLOT * w + T],
                                                     start=True, stop=True)
                            last.then_inc(s_pv, 1)
                        if nxt and p == 0:
                            turn(i, c, 1)
                        if is_unit(u - 1) and p == 3:
                            mix(i, c, 1)

                units(pe, slot)



def by_window(a):
    a = np.asarray(a).reshape(NT, 2, CELLS, WS, CELLS, WS, C)
    return np.ascontiguousarray(a.transpose(0, 1, 2, 4, 3, 5, 6).reshape(NT, P, T, C))


def by_column(*vectors, rows):
    return np.ascontiguousarray(np.stack([np.asarray(v).reshape(-1, rows).T for v in vectors], 2))


def from_units(a):
    tok = np.array(cell_tokens())
    row = (WS * (np.arange(CELLS)[:, None] + tok[:, 0]) + tok[:, 2]) % SIDE
    col = (WS * (np.arange(CELLS)[:, None] + tok[:, 1]) + tok[:, 3]) % SIDE
    a = np.asarray(a).reshape(CELLS, IMGS, CELLS, T, C)
    y = np.empty((IMGS, SIDE, SIDE, C), a.dtype)
    y[np.arange(IMGS)[None, :, None, None], row[:, None, None, :], col[None, None, :, :]] = a
    return y


def shape_constants():
    f = np.float32
    part = np.arange(P)
    image_mean = (part[:, None] // WINS == np.arange(2)).astype(f) / WINS
    masks = np.stack([part // HD % 2 == e for e in range(2)], 1)
    tok = np.array(cell_tokens())
    yi = WS * tok[:, 0] + tok[:, 2] - SHIFT
    xi = WS * tok[:, 1] + tok[:, 3] - SHIFT
    rel = (yi[:, None] - yi[None, :] + WS - 1) * (2 * WS - 1) + xi[:, None] - xi[None, :] + WS - 1
    onehot = np.zeros(((2 * WS - 1) ** 2, T, T), f)
    onehot[rel.T, np.arange(T)[:, None], np.arange(T)[None, :]] = 1
    mask = np.zeros((P, 2, 2, T), f)
    for r in range(2):
        for k in range(2):
            for w in range(2):
                apart = np.zeros((T, T), bool)
                if r:
                    apart |= tok[:, None, 0] != tok[None, :, 0]
                if k and w:
                    apart |= tok[:, None, 1] != tok[None, :, 1]
                mask[SLOT * w:SLOT * w + T, r, k] = np.where(apart, -100.0, 0.0)
    return {"image_mean": image_mean, "identity": np.eye(P, dtype=f), "head_masks": masks.astype(f),
            "onehot": onehot, "shift_mask": mask.reshape(P, 4, T)}


def kernel(**inputs):
    import concourse.bacc as bacc
    from concourse.bass_utils import run_bass_kernel_spmd

    def plain(name):
        return np.ascontiguousarray(inputs[name])

    arrays = {"x": by_window(inputs["x"])}
    twice = np.r_[0:C, P:C]
    for name in ("W2", "b2"):
        arrays[name] = plain("L0_conv_" + name)
    for name in ("A", "Bm", "Cm", "W1"):
        arrays[name] = np.ascontiguousarray(np.asarray(inputs["L0_conv_" + name])[twice])
    for name in ("ln1", "ln2"):
        arrays[name] = by_column(*(np.asarray(inputs[f"L0_conv_{name}_{k}"])[twice] for k in "wb"), rows=P)
    arrays["b1"] = by_column(inputs["L0_conv_b1"], rows=P)[:, :, 0]
    columns = np.r_[0:P, C + P:2 * C, P:C, C:C + P, 2 * C:3 * C]
    arrays["qkvT"] = np.ascontiguousarray(np.asarray(inputs["L1_conv_qkv_w"]).T[twice][:, columns])
    arrays["qkv_b"] = by_column(np.asarray(inputs["L1_conv_qkv_b"])[np.r_[columns, 2 * C + P:3 * C]], rows=P)[:, :, 0]
    arrays["projT"] = np.ascontiguousarray(np.asarray(inputs["L1_conv_proj_w"]).T)
    arrays["proj_b"] = plain("L1_conv_proj_b")
    arrays["rpb"] = plain("L1_conv_rpb_table")
    arrays.update(shape_constants())
    nc = bacc.Bacc("TRN2", target_bir_lowering=False, num_devices=1)
    args = {n: nc.dram_tensor("in_" + n, a.shape, fp32, kind="ExternalInput").ap() for n, a in arrays.items()}
    out = nc.dram_tensor("out", (UNITS, UP, 2, T, C), fp32, kind="ExternalOutput").ap()
    build(nc, **args, out=out)
    r = run_bass_kernel_spmd(nc, [{"in_" + n: a for n, a in arrays.items()}], core_ids=[0])
    return from_units(r.results[0]["out"])
```
